# Optimizing a Trainium2 kernel written in Bass

```python
import numpy as np
import jax
import jax.numpy as jnp

def _softmax(x, axis=-1):
    return jax.nn.softmax(x, axis=axis)

def _gelu(x):
    return jax.nn.gelu(x, approximate=True)

def _silu(x):
    return jax.nn.silu(x)

def _sigmoid(x):
    return jax.nn.sigmoid(x)

def _layernorm(x, axis=-1, eps=1e-05):
    m = jnp.mean(x, axis=axis, keepdims=True)
    v = jnp.var(x, axis=axis, keepdims=True)
    return (x - m) / jnp.sqrt(v + eps)

def _scatter_add(tgt, idx, src, axis=0):
    return tgt.at[idx].add(src)

def _segment_sum(src, seg, n):
    return jax.ops.segment_sum(src, seg, n)
kernel_name = 'mk_prb_d1_jaxref_r8_a4a056'

def setup_inputs(seed: int=0):
    np.random.seed(seed)
    _w = jnp.asarray

    def _L0_attn_setup():
        import math
        import jax, jax.numpy as jnp
        import numpy as np
        NUM_HEADS = 16
        D_MODEL = 128
        D_HEAD = 64
        D_SEQ = 256
        NUM_LAYERS = 24
        BATCH = 2
        key = jax.random.key(seed)
        ks = jax.random.split(key, 10)
        s = math.sqrt(0.02)
        residual = jax.random.normal(ks[0], (BATCH, D_SEQ, D_MODEL), dtype=jnp.float32)
        W_Q = jax.random.normal(ks[1], (NUM_HEADS, D_MODEL, D_HEAD), dtype=jnp.float32) * s
        W_K = jax.random.normal(ks[2], (NUM_HEADS, D_MODEL, D_HEAD), dtype=jnp.float32) * s
        W_V = jax.random.normal(ks[3], (NUM_HEADS, D_MODEL, D_HEAD), dtype=jnp.float32) * s
        W_O = jax.random.normal(ks[4], (NUM_HEADS * D_HEAD, D_MODEL), dtype=jnp.float32) * s
        W_O = W_O / math.sqrt(NUM_LAYERS)
        b_Q = jax.random.normal(ks[5], (NUM_HEADS, D_HEAD), dtype=jnp.float32) * s
        b_K = jax.random.normal(ks[6], (NUM_HEADS, D_HEAD), dtype=jnp.float32) * s
        b_V = jax.random.normal(ks[7], (NUM_HEADS, D_HEAD), dtype=jnp.float32) * s
        b_O = jax.random.normal(ks[8], (D_MODEL,), dtype=jnp.float32) * s
        return dict(residual=residual, W_Q=W_Q, W_K=W_K, W_V=W_V, W_O=W_O, b_Q=b_Q, b_K=b_K, b_V=b_V, b_O=b_O)
    _L0_attn_in = _L0_attn_setup()

    def _L0_ffn_setup():
        import jax, jax.numpy as jnp
        import numpy as np
        D_MODEL = 128
        DEPTH = 8
        M = 2 ** DEPTH
        N_INTERNAL = M - 1
        B, T = (8, 512)

        def _leaf_probs(gate):
            BT = gate.shape[0]
            lp = jnp.ones((BT, M), dtype=gate.dtype)
            for level in range(DEPTH):
                n = 2 ** level
                half = M // (2 * n)
                g = gate[:, n - 1:2 * n - 1]
                f = jnp.stack([1.0 - g, g], axis=-1)
                f = jnp.broadcast_to(f[..., None], (BT, n, 2, half))
                lp = lp * f.reshape(BT, M)
            return lp
        key = jax.random.key(seed)
        ks = jax.random.split(key, 7)
        x = jax.random.normal(ks[0], (B, T, D_MODEL), dtype=jnp.float32)
        Wq = jax.random.normal(ks[1], (D_MODEL, D_MODEL), dtype=jnp.float32) * 0.02
        routers = jax.random.normal(ks[2], (N_INTERNAL, D_MODEL), dtype=jnp.float32) * 0.02
        leaf_keys = jax.random.normal(ks[3], (M, D_MODEL), dtype=jnp.float32) * 0.02
        leaf_values = jax.random.normal(ks[4], (M, D_MODEL), dtype=jnp.float32) * 0.02
        Wout_w = jax.random.normal(ks[5], (D_MODEL, D_MODEL), dtype=jnp.float32) * 0.02
        Wout_b = jax.random.normal(ks[6], (D_MODEL,), dtype=jnp.float32) * 0.02
        return {'x': x, 'Wq': Wq, 'routers': routers, 'leaf_keys': leaf_keys, 'leaf_values': leaf_values, 'Wout_w': Wout_w, 'Wout_b': Wout_b}
    _L0_ffn_in = _L0_ffn_setup()
    _d = {'L0_attn_residual': _L0_attn_in['residual'], 'L0_attn_W_Q': _L0_attn_in['W_Q'], 'L0_attn_W_K': _L0_attn_in['W_K'], 'L0_attn_W_V': _L0_attn_in['W_V'], 'L0_attn_W_O': _L0_attn_in['W_O'], 'L0_attn_b_Q': _L0_attn_in['b_Q'], 'L0_attn_b_K': _L0_attn_in['b_K'], 'L0_attn_b_V': _L0_attn_in['b_V'], 'L0_attn_b_O': _L0_attn_in['b_O'], 'L0_ffn_Wq': _L0_ffn_in['Wq'], 'L0_ffn_routers': _L0_ffn_in['routers'], 'L0_ffn_leaf_keys': _L0_ffn_in['leaf_keys'], 'L0_ffn_leaf_values': _L0_ffn_in['leaf_values'], 'L0_ffn_Wout_w': _L0_ffn_in['Wout_w'], 'L0_ffn_Wout_b': _L0_ffn_in['Wout_b']}
    _x0 = _d['L0_attn_residual']
    _d['L0_attn_residual'] = jax.random.normal(jax.random.fold_in(jax.random.key(seed), 1), (32, 256, 128), dtype=_x0.dtype)
    del _x0
    return _d

def reference(L0_attn_residual, L0_attn_W_Q, L0_attn_W_K, L0_attn_W_V, L0_attn_W_O, L0_attn_b_Q, L0_attn_b_K, L0_attn_b_V, L0_attn_b_O, L0_ffn_Wq, L0_ffn_routers, L0_ffn_leaf_keys, L0_ffn_leaf_values, L0_ffn_Wout_w, L0_ffn_Wout_b):

    def _L0_attn_ref(residual, W_Q, W_K, W_V, W_O, b_Q, b_K, b_V, b_O):
        import math
        import jax, jax.numpy as jnp
        import numpy as np
        NUM_HEADS = 16
        D_MODEL = 128
        D_HEAD = 64
        D_SEQ = 256
        NUM_LAYERS = 24
        BATCH = 2
        Q = jnp.einsum('hmd,bsm->bshd', W_Q, residual) + b_Q
        K = jnp.einsum('hmd,bsm->bshd', W_K, residual) + b_K
        V = jnp.einsum('hmd,bsm->bshd', W_V, residual) + b_V
        QK = jnp.einsum('bqhd,bkhd->bhqk', Q, K)
        seq = residual.shape[1]
        causal = jnp.triu(jnp.ones((seq, seq), dtype=bool), k=1)
        QK_masked = jnp.where(causal, -jnp.inf, QK)
        soft = jax.nn.softmax(QK_masked / math.sqrt(D_HEAD), axis=-1)
        attn = jnp.einsum('bhqk,bkhd->bqhd', soft, V)
        multi_head = attn.reshape(attn.shape[0], attn.shape[1], NUM_HEADS * D_HEAD)
        return jnp.einsum('em,bqe->bqm', W_O, multi_head) + b_O

    def _L0_ffn_ref(x, Wq, routers, leaf_keys, leaf_values, Wout_w, Wout_b):
        import jax, jax.numpy as jnp
        import numpy as np
        D_MODEL = 128
        DEPTH = 8
        M = 2 ** DEPTH
        N_INTERNAL = M - 1
        B, T = (8, 512)

        def _leaf_probs(gate):
            BT = gate.shape[0]
            lp = jnp.ones((BT, M), dtype=gate.dtype)
            for level in range(DEPTH):
                n = 2 ** level
                half = M // (2 * n)
                g = gate[:, n - 1:2 * n - 1]
                f = jnp.stack([1.0 - g, g], axis=-1)
                f = jnp.broadcast_to(f[..., None], (BT, n, 2, half))
                lp = lp * f.reshape(BT, M)
            return lp
        Bv, Tv, d = x.shape
        q = jnp.einsum('btd,ed->bte', x, Wq)
        q_flat = q.reshape(Bv * Tv, d)
        gate = jax.nn.sigmoid(q_flat @ routers.T)
        leaf_prob = _leaf_probs(gate)
        ret = (leaf_prob @ leaf_values).reshape(Bv, Tv, d)
        return jnp.einsum('btd,ed->bte', ret, Wout_w) + Wout_b
    x = L0_attn_residual
    xn = _layernorm(x, axis=-1)
    x = x + _L0_attn_ref(xn, L0_attn_W_Q, L0_attn_W_K, L0_attn_W_V, L0_attn_W_O, L0_attn_b_Q, L0_attn_b_K, L0_attn_b_V, L0_attn_b_O) + _L0_ffn_ref(xn, L0_ffn_Wq, L0_ffn_routers, L0_ffn_leaf_keys, L0_ffn_leaf_values, L0_ffn_Wout_w, L0_ffn_Wout_b)
    return x

_drawn_inputs = setup_inputs


def setup_inputs(seed=0):
    import zlib

    import numpy as np

    out = dict(_drawn_inputs(seed))
    spreads = {}
    factors = {'L0_attn_b_K': 8.0,
     'L0_ffn_Wq': 8.0,
     'L0_ffn_routers': 8.0,
     'L0_ffn_leaf_values': 8.0,
     'L0_ffn_Wout_w': 8.0,
     'L0_ffn_Wout_b': 3.337}
    for name, (base, spread) in spreads.items():
        noise = np.random.default_rng([zlib.crc32(name.encode()), seed]).standard_normal(out[name].shape)
        drawn = base * np.exp(spread * noise) if base else spread * noise
        out[name] = jnp.asarray(drawn.astype(out[name].dtype))
    for name, factor in factors.items():
        out[name] = (out[name] * factor).astype(out[name].dtype)
    return out
```

```python
import concourse.bass as bass
from concourse import mybir
from contextlib import ExitStack


def attention_and_tree_ffn(nc, x, wq_t, wk_t, wv, wo, bq_t, bk_t, bv, bo, ffn_wq, routers_t,
                           leaf_values_t, wout_t, wout_b, out):
    f32 = mybir.dt.float32
    f32r = mybir.dt.float32r
    ALU = mybir.AluOpType
    ACT = mybir.ActivationFunctionType

    BATCH, SEQ, DM = x.shape
    DH, HEADS, _ = wq_t.shape
    P = 128
    QT = SEQ // P
    PAIRS = HEADS // 2
    E = HEADS * DH
    NODES = routers_t.shape[1]
    LEAVES = NODES + 1
    DEPTH = LEAVES.bit_length() - 1
    LC = LEAVES // P
    SCALE = float(DH) ** -0.5
    EPS = 1e-5
    BLOCKS = 3 * P
    MASKED = -3.0e38
    VH = 512
    VQ = QT * E // VH
    PBUF = 4

    SLOTS = BATCH * PAIRS
    LOOP = 2 * PAIRS
    FIRST, START = 1 - PAIRS, PAIRS
    TURNS = (SLOTS - START) // LOOP
    END = START + TURNS * LOOP
    LAST = SLOTS + 3

    x_v = x.rearrange("b (t p) m -> b p t m", p=P)
    out_v = out.rearrange("b (t p) m -> b p t m", p=P)

    with ExitStack() as ctx:
        def sb(name, shape, dt=f32):
            return ctx.enter_context(nc.sbuf_tensor(name, shape, dt))

        def bank(name):
            return ctx.enter_context(nc.psum_tensor(name, [P, 512], f32))

        def sem(name):
            return ctx.enter_context(nc.semaphore(name))

        wqt = sb("wqt", [DH, HEADS, DM])
        wkt = sb("wkt", [DH, HEADS, DM])
        wv_f = sb("wv_f", [DM, E])
        wo_f = sb("wo_f", [P, PAIRS, DM])
        bqt = sb("bqt", [DH, HEADS])
        bkt = sb("bkt", [DH, HEADS])
        bv_b = sb("bv_b", [P, E])
        bo_b = sb("bo_b", [P, DM])
        wb_b = sb("wb_b", [P, DM])
        fwq = sb("fwq", [DM, DM])
        rt = sb("rt", [DM, LEAVES])
        lvt = sb("lvt", [DM, LEAVES])
        wot = sb("wot", [DM, DM])
        a_f = sb("a_f", [DM, HEADS, DM])
        a_hi = sb("a_hi", [DM, HEADS, DM], f32r)
        a_lo = sb("a_lo", [DM, HEADS, DM], f32r)
        wv_hi = sb("wv_hi", [DM, E], f32r)
        wv_lo = sb("wv_lo", [DM, E], f32r)
        rw_f = sb("rw_f", [DM, LEAVES])
        rw_hi = sb("rw_hi", [DM, LEAVES], f32r)
        rw_lo = sb("rw_lo", [DM, LEAVES], f32r)
        lw = sb("lw", [P, LC, DM])
        qbias = sb("qbias", [DM, HEADS])
        kbias_f = sb("kbias_f", [DM, HEADS])
        kbias_hi = sb("kbias_hi", [DM, HEADS], f32r)
        kbias_lo = sb("kbias_lo", [DM, HEADS], f32r)
        bqbk = sb("bqbk", [DH, HEADS])
        bqbk_sum = sb("bqbk_sum", [P, QT, HEADS])
        out_bias = sb("out_bias", [P, DM])
        ident = sb("ident", [P, P])
        ones = sb("ones", [P, P])
        mask = sb("mask", [P, BLOCKS])
        xin = [sb(f"xin{i}", [P, QT, DM]) for i in range(2)]
        res = [sb(f"res{i}", [P, QT, DM]) for i in range(2)]
        stats = sb("stats", [P, QT, 6])
        mv = sb("mv", [P, QT, 2])
        var_eps = sb("var_eps", [P, QT])
        minus_half = sb("minus_half", [P, QT])
        eps = sb("eps", [P, QT])
        rstd = sb("rstd", [P, QT])
        xn = sb("xn", [P, QT, DM])
        xt_f = [sb(f"xt_f{i}", [DM, SEQ]) for i in range(2)]
        xt_hi = [sb(f"xt_hi{i}", [DM, SEQ], f32r) for i in range(2)]
        xt_lo = [sb(f"xt_lo{i}", [DM, SEQ], f32r) for i in range(2)]
        row_b = [sb(f"row_b{i}", [P, QT, HEADS]) for i in range(2)]
        row_bs = [sb(f"row_bs{i}", [P, QT, HEADS]) for i in range(2)]
        v_sb = [sb(f"v_sb{i}", [P, QT, E]) for i in range(2)]
        th = sb("th", [P, QT, LEAVES])
        branch = sb("branch", [P, QT, LEAVES, 2])
        prob = [sb(f"prob{i}", [P, QT, LEAVES]) for i in range(2)]
        leaf_t = sb("leaf_t", [P, LC, SEQ])
        t_sb = [sb(f"t_sb{i}", [DM, 2, SEQ]) for i in range(2)]
        top = [sb(f"top{i}", [P, 2, QT]) for i in range(2)]
        top_b = [sb(f"top_b{i}", [P, 2, QT]) for i in range(2)]
        shift = [sb(f"shift{i}", [P, 2, QT]) for i in range(2)]
        total = [sb(f"total{i}", [P, 2, QT]) for i in range(2)]
        inv = [sb(f"inv{i}", [P, 2, QT]) for i in range(2)]
        p_sb = [sb(f"p_sb{i}", [P, 2, BLOCKS]) for i in range(PBUF)]
        pt_sb = [sb(f"pt_sb{i}", [P, 2, BLOCKS]) for i in range(2)]
        at_sb = [sb(f"at_sb{i}", [P, SEQ]) for i in range(2)]

        ps_s = [bank("ps_s0"), bank("ps_s1")]
        ps_p = [bank("ps_p0"), bank("ps_p1")]
        ps_t = bank("ps_t")
        ps_o = bank("ps_o")
        ps_w = bank("ps_w")
        ps_x = bank("ps_x")

        loaded_qk = sem("loaded_qk")
        loaded_rest = sem("loaded_rest")
        const_set = sem("const_set")
        ident_made = sem("ident_made")
        mask_made = sem("mask_made")
        a_made = sem("a_made")
        a_kept = sem("a_kept")
        small_made = sem("small_made")
        rw_made = sem("rw_made")
        lw_made = sem("lw_made")
        lw_kept = sem("lw_kept")
        bqbk_made = sem("bqbk_made")
        setup_copied = sem("setup_copied")
        setup_act = sem("setup_act")
        setup_dve = sem("setup_dve")
        waits_over = sem("waits_over")
        x_in = [sem("x_in0"), sem("x_in1")]
        stored = [sem("stored0"), sem("stored1")]
        half_stats = sem("half_stats")
        stats_made = sem("stats_made")
        var_made = sem("var_made")
        rstd_made = sem("rstd_made")
        xn_made = sem("xn_made")
        res_made = sem("res_made")
        xt_done = sem("xt_done")
        xt_kept = sem("xt_kept")
        xt_split = sem("xt_split")
        row_done = sem("row_done")
        row_kept = sem("row_kept")
        row_scaled = sem("row_scaled")
        v_done = sem("v_done")
        v_kept = sem("v_kept")
        logits_done = sem("logits_done")
        tanh_made = sem("tanh_made")
        branch_made = sem("branch_made")
        level_made = sem("level_made")
        leaf_made = sem("leaf_made")
        leaft_done = sem("leaft_done")
        leaft_kept = sem("leaft_kept")
        sum_done = sem("sum_done")
        out_made = sem("out_made")
        t_done = sem("t_done")
        t_kept = sem("t_kept")
        s_done = [sem("s_done0"), sem("s_done1")]
        top_made = sem("top_made")
        top_b_made = sem("top_b_made")
        shift_made = sem("shift_made")
        exp_done = [sem("exp_done0"), sem("exp_done1")]
        inv_made = sem("inv_made")
        p_scaled = sem("p_scaled")
        pt_done = [sem("pt_done0"), sem("pt_done1")]
        pt_kept = [sem("pt_kept0"), sem("pt_kept1")]
        pv_done = sem("pv_done")
        at_kept = sem("at_kept")
        wo_done = sem("wo_done")

        def count(n, turn, per_turn):
            return n if turn is None else turn * per_turn + n

        def wait(eng, s, n, turn, per_turn):
            if n > 0:
                eng.wait_ge(s, count(n, turn, per_turn))

        def run(eng, slot):
            for g in range(FIRST, START):
                slot(g, None)
            with eng.Fori(0, TURNS) as turn:
                for g in range(START, START + LOOP):
                    slot(g, turn)
            for g in range(END, LAST + 1):
                slot(g, None)

        def is_pair(g):
            return 0 <= g < SLOTS

        def is_row(b):
            return 0 <= b < BATCH

        block = ctx.enter_context(nc.Block())

        @block.sync
        def _(sp):
            def load(dst, src, s):
                sp.dma_start(dst, src).then_inc(s, 16)

            def load_x(b, turn):
                wait(sp, res_made, b - 1, turn, 2)
                row = b if turn is None else turn * 2 + b
                sp.dma_start(xin[b % 2][:], x_v[bass.ds(row, 1)].rearrange("b p t m -> (b p) t m"))\
                    .then_inc(x_in[b % 2], 16)

            def store(b, turn):
                wait(sp, out_made, b + 1, turn, 2)
                row = b if turn is None else turn * 2 + b
                sp.dma_start(out_v[bass.ds(row, 1)].rearrange("b p t m -> (b p) t m"), res[b % 2][:])\
                    .then_inc(stored[b % 2], 16)

            load_x(0, None)
            load(wqt[:], wq_t, loaded_qk)
            load(wkt[:], wk_t, loaded_qk)
            load(bqt[:], bq_t, loaded_qk)
            load(bkt[:], bk_t, loaded_qk)
            load(wv_f[:].rearrange("m (h d) -> m h d", h=HEADS), wv.rearrange("h m d -> m h d"), loaded_rest)
            load(fwq[:], ffn_wq, loaded_rest)
            load(rt[:, 0:NODES], routers_t, loaded_rest)
            load(bv_b[:], bv.rearrange("h d -> (h d)")[None, :].to_broadcast([P, E]), loaded_rest)
            load_x(1, None)
            load(lvt[:], leaf_values_t, loaded_rest)
            load(wot[:], wout_t, loaded_rest)
            load(wo_f[:], wo.rearrange("(c p) m -> p c m", p=P), loaded_rest)
            load(bo_b[:], bo[None, :].to_broadcast([P, DM]), loaded_rest)
            load(wb_b[:], wout_b[None, :].to_broadcast([P, DM]), loaded_rest)
            load_x(2, None)
            turns = (BATCH - 4) // 2
            with sp.Fori(0, turns) as turn:
                for b in range(2):
                    load_x(b + 3, turn)
                    store(b, turn)
            for b in range(2 * turns, BATCH):
                if b + 3 < BATCH:
                    load_x(b + 3, None)
                store(b, None)
            for i in range(2):
                sp.wait_ge(stored[i], 16 * BATCH // 2)

        LOADS_QK, LOADS_REST = 4 * 16, 9 * 16

        a_banks = [ps_s[0], ps_s[1], ps_p[0], ps_p[1]]
        AH = 512 // DM

        @block.tensor
        def _(pe):
            def split_product(dst, lhs_hi, lhs_lo, rhs_hi, rhs_lo):
                nc.tensor.matmul(dst, lhs_hi, rhs_hi, start=True, stop=False)
                nc.tensor.matmul(dst, lhs_hi, rhs_lo, start=False, stop=False)
                return nc.tensor.matmul(dst, lhs_lo, rhs_hi, start=False, stop=True)

            pe.wait_ge(loaded_qk, LOADS_QK)
            for n, b in enumerate(a_banks):
                for h in range(AH * n, AH * n + AH):
                    last = nc.tensor.matmul(b[:, (h % AH) * DM:(h % AH + 1) * DM], wqt[:, h, :], wkt[:, h, :],
                                            start=True, stop=True)
                last.then_inc(a_made, 1)
            for h in range(HEADS):
                nc.tensor.matmul(ps_o[:, h:h + 1], wkt[:, h, :], bqt[:, h:h + 1], start=True, stop=True)
                nc.tensor.matmul(ps_o[:, HEADS + h:HEADS + h + 1], wqt[:, h, :], bkt[:, h:h + 1],
                                 start=True, stop=True)
            pe.wait_ge(const_set, 2)
            pe.wait_ge(bqbk_made, 1)
            nc.tensor.matmul(ps_o[:, 2 * HEADS:3 * HEADS], ones[0:DH, :], bqbk[:], start=True, stop=True)\
                .then_inc(small_made, 1)
            pe.wait_ge(loaded_rest, LOADS_REST)
            nc.tensor.matmul(ps_x[:, 0:LEAVES], fwq[:], rt[:], start=True, stop=True).then_inc(rw_made, 1)
            for c in range(LC):
                last = nc.tensor.matmul(ps_t[:, c * DM:(c + 1) * DM], lvt[:, c * P:(c + 1) * P], wot[:],
                                        start=True, stop=True)
            last.then_inc(lw_made, 1)
            pe.wait_ge(ident_made, 1)

            def transpose_probabilities(g, turn):
                wait(pe, p_scaled, g + 1, turn, LOOP)
                for h in range(2):
                    wait(pe, pt_kept[h], g, turn, LOOP)
                    for n in range(BLOCKS // P):
                        last = nc.tensor.transpose(ps_p[h][:, n * P:(n + 1) * P],
                                                   p_sb[g % PBUF][:, h, n * P:(n + 1) * P], ident[:])
                    last.then_inc(pt_done[h], 1)

            def scores(g, turn):
                wait(pe, t_kept, g + 1, turn, LOOP)
                t, xt = t_sb[g % 2], xt_f[g // PAIRS % 2]
                if g == 0:
                    pe.wait_ge(a_kept, 4)
                for h in range(2):
                    wait(pe, exp_done[h], g, turn, LOOP)
                    nc.tensor.matmul(ps_s[h][:, 0:P], t[:, h, 0:P], xt[:, 0:P], start=True, stop=True)
                    nc.tensor.matmul(ps_s[h][:, P:BLOCKS], t[:, h, P:SEQ], xt[:, 0:SEQ],
                                     start=True, stop=True).then_inc(s_done[h], 1)

            def project(g, turn):
                b, n = g // PAIRS, g % PAIRS
                if n == 0:
                    wait(pe, xt_split, b + 1, turn, 2)
                if g == 0:
                    pe.wait_ge(lw_kept, 1)
                wait(pe, t_kept, g, turn, LOOP)
                for h in range(2):
                    last = split_product(ps_t[:, h * SEQ:(h + 1) * SEQ],
                                         a_hi[:, 2 * n + h, :], a_lo[:, 2 * n + h, :],
                                         xt_hi[b % 2][:], xt_lo[b % 2][:])
                last.then_inc(t_done, 1)

            def attend(g, turn):
                b, n = g // PAIRS, g % PAIRS
                if n == 0:
                    wait(pe, v_kept, VQ * (b + 1), turn, 2 * VQ)
                if g == 0:
                    pe.wait_ge(setup_copied, 5)
                for h in range(2):
                    wait(pe, pt_kept[h], g + 1, turn, LOOP)
                wait(pe, at_kept, g, turn, LOOP)
                for k, (lo, hi, q) in enumerate(((0, 2 * P, 0), (2 * P, 3 * P, P))):
                    for h in range(2):
                        col = (2 * n + h) * DH
                        last = nc.tensor.matmul(ps_o[h * DH:(h + 1) * DH, q:SEQ], v_sb[b % 2][:, k, col:col + DH],
                                                pt_sb[g % 2][:, h, lo:hi], start=(k == 0), stop=(k == 1),
                                                skip_group_check=True)
                last.then_inc(pv_done, 1)

            def project_out(g, turn):
                b, n = g // PAIRS, g % PAIRS
                wait(pe, at_kept, g + 1, turn, LOOP)
                if n == 0:
                    wait(pe, out_made, b, turn, 2)
                for t in range(QT):
                    last = nc.tensor.matmul(ps_w[:, t * DM:(t + 1) * DM], at_sb[g % 2][:, t * P:(t + 1) * P],
                                            wo_f[:, n, :], start=(n == 0 and t == 0), stop=False,
                                            skip_group_check=True)
                last.then_inc(wo_done, 1)

            def gate_logits(b, turn):
                wait(pe, v_kept, VQ * (b + 1), turn, 2 * VQ)
                for t in range(QT):
                    q = slice(t * P, (t + 1) * P)
                    last = split_product(ps_x[:, t * LEAVES:(t + 1) * LEAVES], xt_hi[b % 2][:, q],
                                         xt_lo[b % 2][:, q], rw_hi[:], rw_lo[:])
                last.then_inc(logits_done, 1)

            def transpose_leaves(b, turn):
                wait(pe, leaf_made, b + 1, turn, 2)
                wait(pe, tanh_made, min(b + 2, BATCH), turn, 2)
                for c in range(LC):
                    for t in range(QT):
                        last = nc.tensor.transpose(ps_x[:, c * SEQ + t * P:c * SEQ + (t + 1) * P],
                                                   prob[DEPTH % 2][:, t, c * P:(c + 1) * P], ident[:])
                last.then_inc(leaft_done, 1)

            def leaves_out(b, turn):
                wait(pe, leaft_kept, b + 1, turn, 2)
                for t in range(QT):
                    for c in range(LC):
                        last = nc.tensor.matmul(ps_w[:, t * DM:(t + 1) * DM], leaf_t[:, c, t * P:(t + 1) * P],
                                                lw[:, c, :], start=False, stop=(c == LC - 1),
                                                skip_group_check=True)
                last.then_inc(sum_done, 1)

            def transpose_x(b, turn):
                wait(pe, xn_made, b + 1, turn, 2)
                wait(pe, leaft_kept, b - 1, turn, 2)
                if b == 0:
                    pe.wait_ge(setup_act, 1)
                for t in range(QT):
                    last = nc.tensor.transpose(ps_x[:, t * P:(t + 1) * P], xn[:, t, :], ident[:])
                last.then_inc(xt_done, 1)

            def row_bias(b, turn):
                wait(pe, xt_split, b + 1, turn, 2)
                if b == 0:
                    pe.wait_ge(setup_dve, 1)
                for t in range(QT):
                    q = slice(t * P, (t + 1) * P)
                    last = split_product(ps_x[:, t * HEADS:(t + 1) * HEADS], xt_hi[b % 2][:, q],
                                         xt_lo[b % 2][:, q], kbias_hi[:], kbias_lo[:])
                last.then_inc(row_done, 1)

            def values(b, j, turn):
                wait(pe, row_kept, b + 1, turn, 2)
                wait(pe, v_kept, VQ * b + j, turn, 2 * VQ)
                t, c = j // (E // VH), j % (E // VH)
                q = slice(t * P, (t + 1) * P)
                split_product(ps_x[:], xt_hi[b % 2][:, q], xt_lo[b % 2][:, q], wv_hi[:, c * VH:(c + 1) * VH],
                              wv_lo[:, c * VH:(c + 1) * VH]).then_inc(v_done, 1)

            def slot(g, turn):
                b, n = g // PAIRS, g % PAIRS
                if is_pair(g - 2):
                    transpose_probabilities(g - 2, turn)
                if n == 3 and is_row(b + 1):
                    transpose_x(b + 1, turn)
                if is_pair(g):
                    scores(g, turn)
                if is_pair(g + 1):
                    project(g + 1, turn)
                if is_pair(g - 2):
                    attend(g - 2, turn)
                if is_pair(g - 3):
                    project_out(g - 3, turn)
                if n == 0 and is_row(b):
                    gate_logits(b, turn)
                if n == 1 and is_row(b - 1):
                    transpose_leaves(b - 1, turn)
                if n == 2 and is_row(b - 1):
                    leaves_out(b - 1, turn)
                if n == 3 and is_row(b + 1):
                    row_bias(b + 1, turn)
                if n >= 4 and is_row(b + 1):
                    values(b + 1, n - 4, turn)

            run(pe, slot)

        @block.vector
        def _(dve):
            V = nc.vector

            V.memset(rt[:, NODES:LEAVES], 0.0)
            V.memset(ones[:], 1.0).then_inc(const_set, 1)
            dve.wait_ge(loaded_qk, LOADS_QK)
            V.tensor_tensor(bqbk[:], bqt[:], bkt[:], ALU.mult).then_inc(bqbk_made, 1)
            for n, b in enumerate(a_banks):
                h = slice(AH * n, AH * n + AH)
                dve.wait_ge(a_made, n + 1)
                V.tensor_copy(a_f[:, h, :].rearrange("p h m -> p (h m)"), b[:]).then_inc(a_kept, 1)
                dve.wait_ge(a_kept, n + 1)
                V.tensor_copy(a_hi[:, h, :], a_f[:, h, :]).then_inc(setup_copied, 1)
                dve.wait_ge(setup_copied, n + 1)
                V.tensor_tensor(a_lo[:, h, :], a_f[:, h, :], a_hi[:, h, :].bitcast(f32), ALU.subtract)
            dve.wait_ge(small_made, 1)
            V.tensor_copy(qbias[:], ps_o[:, 0:HEADS])
            for t in range(QT):
                V.tensor_copy(bqbk_sum[:, t, :], ps_o[:, 2 * HEADS:3 * HEADS])
            V.tensor_copy(kbias_f[:], ps_o[:, HEADS:2 * HEADS]).then_inc(setup_copied, 1)
            dve.wait_ge(setup_copied, 5)
            V.tensor_copy(kbias_hi[:], kbias_f[:]).then_inc(setup_copied, 1)
            dve.wait_ge(setup_copied, 6)
            V.tensor_tensor(kbias_lo[:], kbias_f[:], kbias_hi[:].bitcast(f32), ALU.subtract)
            dve.wait_ge(loaded_rest, LOADS_REST)
            V.tensor_tensor(out_bias[:], bo_b[:], wb_b[:], ALU.add)
            V.tensor_copy(wv_hi[:], wv_f[:]).then_inc(setup_copied, 1)
            dve.wait_ge(setup_copied, 7)
            V.tensor_tensor(wv_lo[:], wv_f[:], wv_hi[:].bitcast(f32), ALU.subtract)
            dve.wait_ge(setup_act, 1)
            V.tensor_copy(rw_hi[:], rw_f[:]).then_inc(setup_copied, 1)
            dve.wait_ge(setup_copied, 8)
            V.tensor_tensor(rw_lo[:], rw_f[:], rw_hi[:].bitcast(f32), ALU.subtract).then_inc(setup_dve, 1)
            dve.wait_ge(mask_made, 1)

            def keep_transposed(g, turn):
                wait(dve, pt_done[0], g + 1, turn, LOOP)
                wait(dve, pv_done, g - 1, turn, LOOP)
                V.tensor_copy(pt_sb[g % 2][:, 0, :], ps_p[0][:, 0:BLOCKS]).then_inc(pt_kept[0], 1)

            def invert_totals(g, turn):
                wait(dve, exp_done[0], g + 1, turn, LOOP)
                wait(dve, exp_done[1], g + 1, turn, LOOP)
                wait(dve, p_scaled, g - 1, turn, LOOP)
                V.reciprocal(inv[g % 2][:], total[g % 2][:]).then_inc(inv_made, 1)

            def mask_and_shift(g, turn):
                b, n, i = g // PAIRS, g % PAIRS, g % 2
                wait(dve, exp_done[1], g - 1, turn, LOOP)
                if n == 0:
                    wait(dve, row_scaled, b + 1, turn, 2)
                for h in range(2):
                    wait(dve, s_done[h], g + 1, turn, LOOP)
                    dve.sem_inc(waits_over, 1)
                    for t, (lo, hi) in enumerate(((0, P), (P, BLOCKS))):
                        last = V.tensor_tensor_reduce(ps_s[h][:, lo:hi], ps_s[h][:, lo:hi], mask[:, lo:hi],
                                                      1.0, MASKED, ALU.add, ALU.max, top[i][:, h, t:t + 1])
                    last.then_inc(top_made, 1)
                    row = row_b[b % 2][:, :, 2 * n + h]
                    rows = row_bs[b % 2][:, :, 2 * n + h]
                    dve.wait_ge(top_made, count(2 * g + h + 1, turn, 2 * LOOP))
                    V.tensor_tensor(top_b[i][:, h, :], top[i][:, h, :], row, ALU.add).then_inc(top_b_made, 1)
                    dve.wait_ge(top_b_made, count(2 * g + h + 1, turn, 2 * LOOP))
                    V.scalar_tensor_tensor(shift[i][:, h, :], top_b[i][:, h, :], -SCALE, rows,
                                           ALU.mult, ALU.add).then_inc(shift_made, 1)

            def keep_projected(g, turn):
                n = g % PAIRS
                wait(dve, t_done, g + 1, turn, LOOP)
                wait(dve, s_done[1], g - 1, turn, LOOP)
                for h in range(2):
                    last = V.tensor_scalar(t_sb[g % 2][:, h, :], ps_t[:, h * SEQ:(h + 1) * SEQ],
                                           qbias[:, 2 * n + h:2 * n + h + 1], None, ALU.add)
                last.then_inc(t_kept, 1)

            def row_stats(b, turn):
                wait(dve, x_in[b % 2], 16 * (b // 2 + 1), turn, 16)
                wait(dve, xn_made, b, turn, 2)
                for t in range(QT):
                    last = V.bn_stats(stats[:, t, :], xin[b % 2][:, t, :])
                last.then_inc(half_stats, 1)
                wait(dve, half_stats, b + 1, turn, 2)
                dve.sem_inc(waits_over, 1)
                for t in range(QT):
                    last = V.bn_aggr(mv[:, t, :], stats[:, t, :])
                last.then_inc(stats_made, 1)

            def normalize(b, turn):
                wait(dve, rstd_made, b + 1, turn, 2)
                wait(dve, stats_made, b + 1, turn, 2)
                wait(dve, xt_done, b, turn, 2)
                for t in range(QT):
                    last = V.tensor_scalar(xn[:, t, :], xin[b % 2][:, t, :], mv[:, t, 0:1], rstd[:, t:t + 1],
                                           ALU.subtract, ALU.mult)
                last.then_inc(xn_made, 1)

            def keep_xt(b, turn):
                i = b % 2
                wait(dve, xt_done, b + 1, turn, 2)
                wait(dve, s_done[1], PAIRS * (b - 1), turn, LOOP)
                V.tensor_copy(xt_f[i][:], ps_x[:, 0:SEQ]).then_inc(xt_kept, 1)
                wait(dve, xt_kept, 2 * b + 1, turn, 4)
                V.tensor_copy(xt_hi[i][:], xt_f[i][:]).then_inc(xt_kept, 1)
                wait(dve, xt_kept, 2 * b + 2, turn, 4)
                V.tensor_tensor(xt_lo[i][:], xt_f[i][:], xt_hi[i][:].bitcast(f32), ALU.subtract)\
                    .then_inc(xt_split, 1)

            def keep_row_bias(b, turn):
                i = b % 2
                wait(dve, row_done, b + 1, turn, 2)
                if b >= 2:
                    wait(dve, shift_made, 2 * PAIRS * (b - 1), turn, 2 * LOOP)
                V.tensor_tensor(row_b[i][:], ps_x[:, 0:QT * HEADS].rearrange("p (t h) -> p t h", t=QT),
                                bqbk_sum[:], ALU.add).then_inc(row_kept, 1)
                wait(dve, row_kept, b + 1, turn, 2)
                V.tensor_scalar(row_bs[i][:], row_b[i][:], SCALE, None, ALU.mult).then_inc(row_scaled, 1)

            def keep_values(b, j, turn):
                t, c = j // (E // VH), j % (E // VH)
                wait(dve, v_done, VQ * b + j + 1, turn, 2 * VQ)
                wait(dve, pv_done, PAIRS * (b - 1), turn, LOOP)
                V.tensor_tensor(v_sb[b % 2][:, t, c * VH:(c + 1) * VH], ps_x[:], bv_b[:, c * VH:(c + 1) * VH],
                                ALU.add).then_inc(v_kept, 1)

            def finish(b, turn):
                wait(dve, sum_done, b + 1, turn, 2)
                wait(dve, wo_done, PAIRS * (b + 1), turn, LOOP)
                wait(dve, res_made, b + 1, turn, 2)
                r = res[b % 2][:].rearrange("p t m -> p (t m)")
                V.tensor_tensor(r, ps_w[:, 0:QT * DM], r, ALU.add).then_inc(out_made, 1)

            def slot(g, turn):
                b, n = g // PAIRS, g % PAIRS
                if is_pair(g - 2):
                    keep_transposed(g - 2, turn)
                if is_pair(g - 1):
                    invert_totals(g - 1, turn)
                if n == 3 and is_row(b - 1):
                    finish(b - 1, turn)
                if n == 3 and is_row(b + 1):
                    keep_xt(b + 1, turn)
                if n == 4 and is_row(b + 1):
                    keep_row_bias(b + 1, turn)
                if n >= 5 and is_row(b + 1):
                    keep_values(b + 1, n - 5, turn)
                if n == 0 and is_row(b):
                    keep_values(b, VQ - 1, turn)
                if is_pair(g):
                    mask_and_shift(g, turn)
                if is_pair(g + 1) and g % 2 == 0:
                    keep_projected(g + 1, turn)
                if n == 1 and is_row(b + 1):
                    row_stats(b + 1, turn)
                if n == 2 and is_row(b + 1):
                    normalize(b + 1, turn)

            run(dve, slot)

        @block.scalar
        def _(act):
            A = nc.scalar

            act.wait_ge(rw_made, 1)
            A.activation(rw_f[:], ps_x[:, 0:LEAVES], ACT.Copy).then_inc(setup_act, 1)
            act.wait_ge(lw_made, 1)
            A.activation(lw[:].rearrange("p c m -> p (c m)"), ps_t[:, 0:LC * DM], ACT.Copy,
                         scale=float(0.5 ** DEPTH)).then_inc(lw_kept, 1)
            act.wait_ge(setup_copied, 5)

            def keep_transposed(g, turn):
                wait(act, pt_done[1], g + 1, turn, LOOP)
                wait(act, pv_done, g - 1, turn, LOOP)
                A.activation(pt_sb[g % 2][:, 1, :], ps_p[1][:, 0:BLOCKS], ACT.Copy).then_inc(pt_kept[1], 1)

            def exponentials(g, turn):
                i = g % 2
                wait(act, pt_done[1], g - PBUF + 1, turn, LOOP)
                wait(act, inv_made, g - 1, turn, LOOP)
                for h in range(2):
                    act.wait_ge(shift_made, count(2 * g + h + 1, turn, 2 * LOOP))
                    for t, (lo, hi) in enumerate(((0, P), (P, BLOCKS))):
                        last = A.activation(p_sb[g % PBUF][:, h, lo:hi], ps_s[h][:, lo:hi], ACT.Exp,
                                            bias=shift[i][:, h, t:t + 1], scale=SCALE,
                                            accum_out=total[i][:, h, t:t + 1])
                    last.then_inc(exp_done[h], 1)

            def keep_projected(g, turn):
                n = g % PAIRS
                wait(act, t_done, g + 1, turn, LOOP)
                wait(act, s_done[1], g - 1, turn, LOOP)
                for h in range(2):
                    last = A.activation(t_sb[g % 2][:, h, :], ps_t[:, h * SEQ:(h + 1) * SEQ], ACT.Identity,
                                        bias=qbias[:, 2 * n + h:2 * n + h + 1])
                last.then_inc(t_kept, 1)

            def keep_attended(g, turn):
                wait(act, pv_done, g + 1, turn, LOOP)
                wait(act, wo_done, g - 1, turn, LOOP)
                A.activation(at_sb[g % 2][:], ps_o[:, 0:SEQ], ACT.Copy).then_inc(at_kept, 1)

            def gates(b, turn):
                wait(act, logits_done, b + 1, turn, 2)
                wait(act, branch_made, b, turn, 2)
                A.activation(th[:].rearrange("p t n -> p (t n)"), ps_x[:], ACT.Tanh, scale=0.5)\
                    .then_inc(tanh_made, 1)

            def keep_leaves(b, turn):
                wait(act, leaft_done, b + 1, turn, 2)
                wait(act, sum_done, b, turn, 2)
                A.activation(leaf_t[:].rearrange("p c q -> p (c q)"), ps_x[:], ACT.Copy).then_inc(leaft_kept, 1)

            def slot(g, turn):
                b, n = g // PAIRS, g % PAIRS
                if is_pair(g - 2):
                    keep_transposed(g - 2, turn)
                if n == 1 and is_row(b):
                    gates(b, turn)
                if n == 2 and is_row(b - 1):
                    keep_leaves(b - 1, turn)
                if is_pair(g):
                    exponentials(g, turn)
                if is_pair(g + 1) and g % 2 == 1:
                    keep_projected(g + 1, turn)
                if is_pair(g - 2):
                    keep_attended(g - 2, turn)

            run(act, slot)

        @block.gpsimd
        def _(pool):
            G = nc.gpsimd

            G.memset(ident[:], 0.0)
            G.memset(minus_half[:], -0.5)
            G.memset(eps[:], EPS)
            G.memset(mask[:], 0.0).then_inc(const_set, 1)
            pool.wait_ge(const_set, 2)
            G.affine_select(out=ident[:], in_=ident[:], compare_op=ALU.not_equal, fill=1.0, base=0,
                            pattern=[[-1, P]], channel_multiplier=1).then_inc(ident_made, 1)
            G.affine_select(out=mask[:, 0:P], in_=mask[:, 0:P], compare_op=ALU.is_ge, fill=MASKED, base=0,
                            pattern=[[-1, P]], channel_multiplier=1)
            G.affine_select(out=mask[:, 2 * P:3 * P], in_=mask[:, 2 * P:3 * P], compare_op=ALU.is_ge,
                            fill=MASKED, base=0, pattern=[[-1, P]], channel_multiplier=1).then_inc(mask_made, 1)
            pool.wait_ge(setup_dve, 1)

            def scale_probabilities(g, turn):
                wait(pool, inv_made, g + 1, turn, LOOP)
                p, r = p_sb[g % PBUF], inv[g % 2]
                for t, (lo, hi) in enumerate(((0, P), (P, BLOCKS))):
                    last = G.tensor_tensor(p[:, :, lo:hi], p[:, :, lo:hi],
                                           r[:, :, t:t + 1].to_broadcast([P, 2, hi - lo]), ALU.mult)
                last.then_inc(p_scaled, 1)

            def reciprocal_deviation(b, turn):
                wait(pool, stats_made, b + 1, turn, 2)
                wait(pool, xn_made, b, turn, 2)
                G.tensor_tensor(var_eps[:], mv[:, :, 1], eps[:], ALU.add).then_inc(var_made, 1)
                wait(pool, var_made, b + 1, turn, 2)
                G.tensor_tensor(rstd[:], var_eps[:], minus_half[:], ALU.pow).then_inc(rstd_made, 1)

            def branches(b, turn):
                wait(pool, tanh_made, b + 1, turn, 2)
                one = ones[:, 0:1, None].to_broadcast([P, QT, LEAVES])
                G.tensor_tensor(branch[:, :, :, 0], one, th[:], ALU.subtract)
                G.tensor_tensor(branch[:, :, :, 1], one, th[:], ALU.add).then_inc(branch_made, 1)

            def tree_levels(b, levels, turn):
                for level in levels:
                    n = 2 ** level
                    if level == 1:
                        wait(pool, branch_made, b + 1, turn, 2)
                        parent = branch[:, :, 0, :]
                        wait(pool, leaft_done, b, turn, 2)
                    else:
                        parent = prob[level % 2][:, :, 0:n]
                        pool.wait_ge(level_made, count((DEPTH - 2) * b + level - 1, turn, 2 * (DEPTH - 2)))
                    last = G.tensor_tensor(
                        prob[(level + 1) % 2][:, :, 0:2 * n].rearrange("p t (n c) -> p t n c", c=2),
                        parent[:, :, :, None].to_broadcast([P, QT, n, 2]),
                        branch[:, :, n - 1:2 * n - 1, :], ALU.mult)
                    if level < DEPTH - 1:
                        last.then_inc(level_made, 1)
                    else:
                        last.then_inc(leaf_made, 1)

            def residual(b, turn):
                wait(pool, x_in[b % 2], 16 * (b // 2 + 1), turn, 16)
                wait(pool, xn_made, b + 1, turn, 2)
                wait(pool, stored[b % 2], 16 * (b // 2), turn, 16)
                G.tensor_tensor(res[b % 2][:], xin[b % 2][:],
                                out_bias[:, None, :].to_broadcast([P, QT, DM]), ALU.add).then_inc(res_made, 1)

            def slot(g, turn):
                b, n = g // PAIRS, g % PAIRS
                if is_pair(g - 1):
                    scale_probabilities(g - 1, turn)
                if n == 1 and is_row(b + 1):
                    reciprocal_deviation(b + 1, turn)
                if n == 1 and is_row(b):
                    branches(b, turn)
                if n == 2 and is_row(b):
                    tree_levels(b, range(1, 5), turn)
                if n == 3 and is_row(b):
                    tree_levels(b, range(5, DEPTH), turn)
                if n == 5 and is_row(b + 1):
                    residual(b + 1, turn)

            run(pool, slot)


def kernel(**inputs):
    import numpy as np
    import concourse.bacc as bacc
    from concourse.bass_utils import run_bass_kernel_spmd

    def given(name):
        return np.asarray(inputs[name])

    laid_out = {
        "x": given("L0_attn_residual"),
        "wq_t": given("L0_attn_W_Q").transpose(2, 0, 1),
        "wk_t": given("L0_attn_W_K").transpose(2, 0, 1),
        "wv": given("L0_attn_W_V"),
        "wo": given("L0_attn_W_O"),
        "bq_t": given("L0_attn_b_Q").T,
        "bk_t": given("L0_attn_b_K").T,
        "bv": given("L0_attn_b_V"),
        "bo": given("L0_attn_b_O"),
        "ffn_wq": given("L0_ffn_Wq"),
        "routers_t": given("L0_ffn_routers").T,
        "leaf_values_t": given("L0_ffn_leaf_values").T,
        "wout_t": given("L0_ffn_Wout_w").T,
        "wout_b": given("L0_ffn_Wout_b"),
    }
    nc = bacc.Bacc("TRN2", target_bir_lowering=False, num_devices=1)
    arrays, args = {}, []
    for name, a in laid_out.items():
        a = np.ascontiguousarray(a)
        arrays[f"in_{name}"] = a
        args.append(nc.dram_tensor(f"in_{name}", a.shape, mybir.dt.from_np(a.dtype), kind="ExternalInput").ap())
    out = nc.dram_tensor("out", laid_out["x"].shape, mybir.dt.float32, kind="ExternalOutput").ap()
    attention_and_tree_ffn(nc, *args, out)
    result = run_bass_kernel_spmd(nc, [arrays], core_ids=[0])
    return result.results[0]["out"]
```

```python
import concourse.bass as bass
from concourse import mybir
from contextlib import ExitStack


def attention_and_tree_ffn(nc, x, wq_t, wk_t, wv, wo, bq_t, bk_t, bv, bo, ffn_wq, routers_t,
                           leaf_values_t, wout_t, wout_b, out):
    f32 = mybir.dt.float32
    f32r = mybir.dt.float32r
    ALU = mybir.AluOpType
    ACT = mybir.ActivationFunctionType

    BATCH, SEQ, DM = x.shape
    DH, HEADS, _ = wq_t.shape
    P = 128
    QT = SEQ // P
    PAIRS = HEADS // 2
    E = HEADS * DH
    NODES = routers_t.shape[1]
    LEAVES = NODES + 1
    DEPTH = LEAVES.bit_length() - 1
    LC = LEAVES // P
    SCALE = float(DH) ** -0.5
    EPS = 1e-5
    BLOCKS = 3 * P
    MASKED = -3.0e38
    VH = 512
    VQ = QT * E // VH
    PBUF = 4

    SLOTS = BATCH * PAIRS
    LOOP = 2 * PAIRS
    FIRST, START = -PAIRS, PAIRS
    TURNS = (SLOTS - START) // LOOP
    END = START + TURNS * LOOP
    T_LAG, V_LAG, O_LAG = 2, 4, 5
    SUM_SLOT = O_LAG - 1
    LAST = SLOTS + SUM_SLOT + 1
    TWOS = PAIRS // 2

    x_v = x.rearrange("b (t p) m -> b p t m", p=P)
    out_v = out.rearrange("b (t p) m -> b p t m", p=P)

    with ExitStack() as ctx:
        def sb(name, shape, dt=f32):
            return ctx.enter_context(nc.sbuf_tensor(name, shape, dt))

        def bank(name):
            return ctx.enter_context(nc.psum_tensor(name, [P, 512], f32))

        def sem(name):
            return ctx.enter_context(nc.semaphore(name))

        wqt = sb("wqt", [DH, HEADS, DM])
        wkt = sb("wkt", [DH, HEADS, DM])
        wv_f = sb("wv_f", [DM, E])
        wo_f = sb("wo_f", [P, PAIRS, DM])
        bqt = sb("bqt", [DH, HEADS])
        bkt = sb("bkt", [DH, HEADS])
        bv_b = sb("bv_b", [P, E])
        bo_b = sb("bo_b", [P, DM])
        wb_b = sb("wb_b", [P, DM])
        fwq = sb("fwq", [DM, DM])
        rt = sb("rt", [DM, LEAVES])
        lvt = sb("lvt", [DM, LEAVES])
        wot = sb("wot", [DM, DM])
        a_f = sb("a_f", [DM, HEADS, DM])
        a_hi = sb("a_hi", [DM, HEADS, DM], f32r)
        a_lo = sb("a_lo", [DM, HEADS, DM], f32r)
        wv_hi = sb("wv_hi", [DM, E], f32r)
        wv_lo = sb("wv_lo", [DM, E], f32r)
        rw_f = sb("rw_f", [DM, LEAVES])
        rw_hi = sb("rw_hi", [DM, LEAVES], f32r)
        rw_lo = sb("rw_lo", [DM, LEAVES], f32r)
        wo_hi = sb("wo_hi", [P, PAIRS, DM], f32r)
        wo_lo = sb("wo_lo", [P, PAIRS, DM], f32r)
        lw = sb("lw", [P, LC, DM])
        qbias = sb("qbias", [DM, HEADS])
        kbias_f = sb("kbias_f", [DM, HEADS])
        bqbk = sb("bqbk", [DH, HEADS])
        bqbk_sum = sb("bqbk_sum", [P, QT, HEADS])
        out_bias = sb("out_bias", [P, DM])
        ident = sb("ident", [P, P])
        ones = sb("ones", [P, P])
        mask = sb("mask", [P, BLOCKS])
        xin = [sb(f"xin{i}", [P, QT, DM]) for i in range(2)]
        res = [sb(f"res{i}", [P, QT, DM]) for i in range(2)]
        stats = sb("stats", [P, QT, 6])
        mv = sb("mv", [P, QT, 2])
        var_eps = sb("var_eps", [P, QT])
        minus_half = sb("minus_half", [P, QT])
        eps = sb("eps", [P, QT])
        rstd = sb("rstd", [P, QT])
        xn = sb("xn", [P, QT, DM])
        xt_f = [sb(f"xt_f{i}", [DM, SEQ]) for i in range(2)]
        xt_hi = [sb(f"xt_hi{i}", [DM, SEQ], f32r) for i in range(2)]
        xt_lo = [sb(f"xt_lo{i}", [DM, SEQ], f32r) for i in range(2)]
        row_b = sb("row_b", [P, QT, HEADS])
        row_bs = sb("row_bs", [P, QT, HEADS])
        row_d = [sb(f"row_d{i}", [P, QT, HEADS]) for i in range(2)]
        v_sb = [sb(f"v_sb{i}", [P, QT, E]) for i in range(2)]
        th = sb("th", [P, QT, LEAVES])
        branch = sb("branch", [P, QT, LEAVES, 2])
        prob = [sb(f"prob{i}", [P, QT, LEAVES]) for i in range(2)]
        leaf_t = sb("leaf_t", [P, LC, SEQ])
        sum_t = sb("sum_t", [DM, SEQ])
        t_sb = [sb(f"t_sb{i}", [DM, 2, SEQ]) for i in range(2)]
        t_hi = [sb(f"t_hi{i}", [DM, 2, P], f32r) for i in range(2)]
        t_lo = [sb(f"t_lo{i}", [DM, 2, P], f32r) for i in range(2)]
        top = [sb(f"top{i}", [P, 2, QT]) for i in range(2)]
        shift = [sb(f"shift{i}", [P, 2, QT]) for i in range(2)]
        total = [sb(f"total{i}", [P, 2, QT]) for i in range(2)]
        inv = [sb(f"inv{i}", [P, 2, QT]) for i in range(2)]
        p_sb = [sb(f"p_sb{i}", [P, 2, BLOCKS]) for i in range(PBUF)]
        pt_sb = [sb(f"pt_sb{i}", [P, 2, BLOCKS]) for i in range(PBUF)]
        at_hi = [sb(f"at_hi{i}", [P, 2, SEQ], f32r) for i in range(2)]
        at_lo = [sb(f"at_lo{i}", [P, 2, SEQ], f32r) for i in range(2)]

        ps_s = [bank("ps_s0"), bank("ps_s1")]
        ps_p = [bank("ps_p0"), bank("ps_p1")]
        ps_t = bank("ps_t")
        ps_o = bank("ps_o")
        ps_w = bank("ps_w")
        ps_x = bank("ps_x")

        loaded_qk = sem("loaded_qk")
        loaded_rest = sem("loaded_rest")
        const_set = sem("const_set")
        ident_made = sem("ident_made")
        mask_made = sem("mask_made")
        a_made = sem("a_made")
        a_kept = sem("a_kept")
        small_made = sem("small_made")
        rw_made = sem("rw_made")
        lw_made = sem("lw_made")
        lw_kept = sem("lw_kept")
        bqbk_made = sem("bqbk_made")
        setup_copied = sem("setup_copied")
        wo_made = sem("wo_made")
        setup_act = sem("setup_act")
        setup_dve = sem("setup_dve")
        waits_over = sem("waits_over")
        x_in = [sem("x_in0"), sem("x_in1")]
        stored = [sem("stored0"), sem("stored1")]
        half_stats = sem("half_stats")
        stats_made = sem("stats_made")
        var_made = sem("var_made")
        rstd_made = sem("rstd_made")
        xn_made = sem("xn_made")
        res_made = sem("res_made")
        xt_done = sem("xt_done")
        xt_kept = sem("xt_kept")
        xt_split = sem("xt_split")
        row_done = sem("row_done")
        row_kept = sem("row_kept")
        row_scaled = sem("row_scaled")
        v_done = sem("v_done")
        v_kept = sem("v_kept")
        logits_done = sem("logits_done")
        tanh_made = sem("tanh_made")
        branch_made = sem("branch_made")
        level_made = sem("level_made")
        leaf_made = sem("leaf_made")
        leaft_done = sem("leaft_done")
        leaft_kept = sem("leaft_kept")
        leaves_done = sem("leaves_done")
        sum_kept = sem("sum_kept")
        out_done = sem("out_done")
        out_made = sem("out_made")
        t_done = sem("t_done")
        t_kept = sem("t_kept")
        t_rounded = sem("t_rounded")
        t_split = sem("t_split")
        s_done = [sem("s_done0"), sem("s_done1")]
        top_made = sem("top_made")
        shift_made = sem("shift_made")
        exp_done = [sem("exp_done0"), sem("exp_done1")]
        inv_made = sem("inv_made")
        p_scaled = sem("p_scaled")
        pt_done = [sem("pt_done0"), sem("pt_done1")]
        pt_kept = [sem("pt_kept0"), sem("pt_kept1")]
        pv_done = sem("pv_done")
        at_rounded = sem("at_rounded")
        at_split = sem("at_split")
        wo_done = sem("wo_done")

        def count(n, turn, per_turn):
            return n if turn is None else turn * per_turn + n

        def wait(eng, s, n, turn, per_turn):
            if n > 0:
                eng.wait_ge(s, count(n, turn, per_turn))

        def run(eng, slot):
            for g in range(FIRST, START):
                slot(g, None)
            with eng.Fori(0, TURNS) as turn:
                for g in range(START, START + LOOP):
                    slot(g, turn)
            for g in range(END, LAST + 1):
                slot(g, None)

        def is_pair(g):
            return 0 <= g < SLOTS

        def is_row(b):
            return 0 <= b < BATCH

        block = ctx.enter_context(nc.Block())

        @block.sync
        def _(sp):
            def load(dst, src, s):
                sp.dma_start(dst, src).then_inc(s, 16)

            def load_x(b, turn):
                wait(sp, res_made, b - 1, turn, 2)
                row = b if turn is None else turn * 2 + b
                sp.dma_start(xin[b % 2][:], x_v[bass.ds(row, 1)].rearrange("b p t m -> (b p) t m"))\
                    .then_inc(x_in[b % 2], 16)

            def store(b, turn):
                wait(sp, out_made, b + 1, turn, 2)
                row = b if turn is None else turn * 2 + b
                sp.dma_start(out_v[bass.ds(row, 1)].rearrange("b p t m -> (b p) t m"), res[b % 2][:])\
                    .then_inc(stored[b % 2], 16)

            load_x(0, None)
            load(wqt[:], wq_t, loaded_qk)
            load(wkt[:], wk_t, loaded_qk)
            load(bqt[:], bq_t, loaded_qk)
            load(bkt[:], bk_t, loaded_qk)
            load(wv_f[:].rearrange("m (h d) -> m h d", h=HEADS), wv.rearrange("h m d -> m h d"), loaded_rest)
            load(fwq[:], ffn_wq, loaded_rest)
            load(rt[:, 0:NODES], routers_t, loaded_rest)
            load(bv_b[:], bv.rearrange("h d -> (h d)")[None, :].to_broadcast([P, E]), loaded_rest)
            load_x(1, None)
            load(lvt[:], leaf_values_t, loaded_rest)
            load(wot[:], wout_t, loaded_rest)
            load(wo_f[:], wo.rearrange("(c p) m -> p c m", p=P), loaded_rest)
            load(bo_b[:], bo[None, :].to_broadcast([P, DM]), loaded_rest)
            load(wb_b[:], wout_b[None, :].to_broadcast([P, DM]), loaded_rest)
            load_x(2, None)
            turns = (BATCH - 4) // 2
            with sp.Fori(0, turns) as turn:
                for b in range(2):
                    load_x(b + 3, turn)
                    store(b, turn)
            for b in range(2 * turns, BATCH):
                if b + 3 < BATCH:
                    load_x(b + 3, None)
                store(b, None)
            for i in range(2):
                sp.wait_ge(stored[i], 16 * BATCH // 2)

        LOADS_QK, LOADS_REST = 4 * 16, 9 * 16

        a_banks = [ps_s[0], ps_s[1], ps_p[0], ps_p[1]]
        AH = 512 // DM

        @block.tensor
        def _(pe):
            def split_product(dst, lhs_hi, lhs_lo, rhs_hi, rhs_lo):
                nc.tensor.matmul(dst, lhs_hi, rhs_hi, start=True, stop=False)
                nc.tensor.matmul(dst, lhs_hi, rhs_lo, start=False, stop=False)
                return nc.tensor.matmul(dst, lhs_lo, rhs_hi, start=False, stop=True)

            pe.wait_ge(loaded_qk, LOADS_QK)
            for n, b in enumerate(a_banks):
                for h in range(AH * n, AH * n + AH):
                    last = nc.tensor.matmul(b[:, (h % AH) * DM:(h % AH + 1) * DM], wqt[:, h, :], wkt[:, h, :],
                                            start=True, stop=True)
                last.then_inc(a_made, 1)
            for h in range(HEADS):
                nc.tensor.matmul(ps_o[:, h:h + 1], wkt[:, h, :], bqt[:, h:h + 1], start=True, stop=True)
                nc.tensor.matmul(ps_o[:, HEADS + h:HEADS + h + 1], wqt[:, h, :], bkt[:, h:h + 1],
                                 start=True, stop=True)
            pe.wait_ge(const_set, 2)
            pe.wait_ge(bqbk_made, 1)
            nc.tensor.matmul(ps_o[:, 2 * HEADS:3 * HEADS], ones[0:DH, :], bqbk[:], start=True, stop=True)\
                .then_inc(small_made, 1)
            pe.wait_ge(loaded_rest, LOADS_REST)
            nc.tensor.matmul(ps_x[:, 0:LEAVES], fwq[:], rt[:], start=True, stop=True).then_inc(rw_made, 1)
            for c in range(LC):
                last = nc.tensor.matmul(ps_t[:, c * DM:(c + 1) * DM], lvt[:, c * P:(c + 1) * P], wot[:],
                                        start=True, stop=True)
            last.then_inc(lw_made, 1)
            pe.wait_ge(ident_made, 1)

            def transpose_probabilities(g, turn):
                wait(pe, p_scaled, g + 1, turn, LOOP)
                for h in range(2):
                    wait(pe, pt_kept[h], g, turn, LOOP)
                    for n in range(BLOCKS // P):
                        last = nc.tensor.transpose(ps_p[h][:, n * P:(n + 1) * P],
                                                   p_sb[g % PBUF][:, h, n * P:(n + 1) * P], ident[:])
                    last.then_inc(pt_done[h], 1)

            def scores(g, turn):
                wait(pe, t_split, g + 1, turn, LOOP)
                i, b = g % 2, g // PAIRS % 2
                if g == 0:
                    pe.wait_ge(a_kept, 4)
                for h in range(2):
                    wait(pe, exp_done[h], g, turn, LOOP)
                    nc.tensor.matmul(ps_s[h][:, 0:P], t_sb[i][:, h, 0:P], xt_f[b][:, 0:P], start=True, stop=True)
                    split_product(ps_s[h][:, P:BLOCKS], t_hi[i][:, h, :], t_lo[i][:, h, :],
                                  xt_hi[b][:], xt_lo[b][:]).then_inc(s_done[h], 1)

            def project(g, turn):
                b, n = g // PAIRS, g % PAIRS
                if n == 0:
                    wait(pe, xt_split, b + 1, turn, 2)
                if g == 0:
                    pe.wait_ge(lw_kept, 1)
                wait(pe, t_kept, g, turn, LOOP)
                for h in range(2):
                    last = split_product(ps_t[:, h * SEQ:(h + 1) * SEQ],
                                         a_hi[:, 2 * n + h, :], a_lo[:, 2 * n + h, :],
                                         xt_hi[b % 2][:], xt_lo[b % 2][:])
                last.then_inc(t_done, 1)

            def attend(g, turn):
                b, n = g // PAIRS, g % PAIRS
                if n == 0:
                    wait(pe, v_kept, VQ * (b + 1), turn, 2 * VQ)
                if g == 0:
                    pe.wait_ge(setup_copied, 5)
                for h in range(2):
                    wait(pe, pt_kept[h], g + 2, turn, LOOP)
                wait(pe, at_split, g // 2, turn, LOOP // 2)
                for j in range(2):
                    for k, (lo, hi, q) in enumerate(((0, 2 * P, 0), (2 * P, 3 * P, P))):
                        for h in range(2):
                            col = (2 * (n + j) + h) * DH
                            last = nc.tensor.matmul(ps_o[h * DH:(h + 1) * DH, j * SEQ + q:(j + 1) * SEQ],
                                                    v_sb[b % 2][:, k, col:col + DH],
                                                    pt_sb[(g + j) % PBUF][:, h, lo:hi],
                                                    start=(j == 0 and k == 0), stop=(k == 1),
                                                    skip_group_check=True)
                last.then_inc(pv_done, 1)

            def project_out(g, turn):
                b, n, i = g // PAIRS, g % PAIRS, g // 2 % 2
                wait(pe, at_rounded, g // 2 + 1, turn, LOOP // 2)
                if g == 0:
                    pe.wait_ge(wo_made, 1)
                if n == 0:
                    wait(pe, out_made, b, turn, 2)
                for k, (w, at) in enumerate(((wo_hi, at_hi), (wo_lo, at_hi), (wo_hi, at_lo))):
                    if k == 2:
                        wait(pe, at_split, g // 2 + 1, turn, LOOP // 2)
                    for j in range(2):
                        last = nc.tensor.matmul(ps_w[:, 0:SEQ], w[:, n + j, :], at[i][:, j, :],
                                                start=(n + j == 0 and k == 0), stop=(n + j == PAIRS - 1 and k == 2),
                                                skip_group_check=True)
                last.then_inc(wo_done, 1)

            def transpose_out(b, turn):
                wait(pe, sum_kept, b + 1, turn, 2)
                for t in range(QT):
                    last = nc.tensor.transpose(ps_w[:, t * DM:(t + 1) * DM], sum_t[:, t * P:(t + 1) * P], ident[:])
                last.then_inc(out_done, 1)

            def gate_logits(b, turn):
                wait(pe, v_kept, VQ * (b + 1), turn, 2 * VQ)
                for t in range(QT):
                    q = slice(t * P, (t + 1) * P)
                    last = split_product(ps_x[:, t * LEAVES:(t + 1) * LEAVES], xt_hi[b % 2][:, q],
                                         xt_lo[b % 2][:, q], rw_hi[:], rw_lo[:])
                last.then_inc(logits_done, 1)

            def transpose_leaves(b, turn):
                wait(pe, leaf_made, b + 1, turn, 2)
                wait(pe, tanh_made, min(b + 2, BATCH), turn, 2)
                for c in range(LC):
                    for t in range(QT):
                        last = nc.tensor.transpose(ps_x[:, c * SEQ + t * P:c * SEQ + (t + 1) * P],
                                                   prob[DEPTH % 2][:, t, c * P:(c + 1) * P], ident[:])
                last.then_inc(leaft_done, 1)

            def leaves_out(b, turn):
                wait(pe, leaft_kept, b + 1, turn, 2)
                for c in range(LC):
                    last = nc.tensor.matmul(ps_w[:, 0:SEQ], lw[:, c, :], leaf_t[:, c, :], start=False, stop=False,
                                            skip_group_check=True)
                last.then_inc(leaves_done, 1)

            def transpose_x(b, turn):
                wait(pe, xn_made, b + 1, turn, 2)
                wait(pe, leaft_kept, b - 1, turn, 2)
                if b == 0:
                    pe.wait_ge(setup_act, 1)
                for t in range(QT):
                    last = nc.tensor.transpose(ps_x[:, t * P:(t + 1) * P], xn[:, t, :], ident[:])
                last.then_inc(xt_done, 1)

            def row_bias(b, turn):
                wait(pe, xt_split, b + 1, turn, 2)
                if b == 0:
                    pe.wait_ge(setup_dve, 1)
                for t in range(QT):
                    last = nc.tensor.matmul(ps_x[:, t * HEADS:(t + 1) * HEADS], xt_f[b % 2][:, t * P:(t + 1) * P],
                                            kbias_f[:], start=True, stop=True)
                last.then_inc(row_done, 1)

            def values(b, j, turn):
                wait(pe, row_kept, b + 1, turn, 2)
                wait(pe, v_kept, VQ * b + j, turn, 2 * VQ)
                t, c = j // (E // VH), j % (E // VH)
                q = slice(t * P, (t + 1) * P)
                split_product(ps_x[:], xt_hi[b % 2][:, q], xt_lo[b % 2][:, q], wv_hi[:, c * VH:(c + 1) * VH],
                              wv_lo[:, c * VH:(c + 1) * VH]).then_inc(v_done, 1)

            def slot(g, turn):
                b, n = g // PAIRS, g % PAIRS
                if is_pair(g):
                    scores(g, turn)
                if is_pair(g + 2):
                    project(g + 2, turn)
                if is_pair(g - T_LAG):
                    transpose_probabilities(g - T_LAG, turn)
                if n == 0 and is_row(b):
                    gate_logits(b, turn)
                if n == 1 and is_row(b - 1):
                    transpose_leaves(b - 1, turn)
                if n == 2 and is_row(b + 1):
                    transpose_x(b + 1, turn)
                if n == 3 and is_row(b + 1):
                    row_bias(b + 1, turn)
                if n >= 4 and is_row(b + 1):
                    values(b + 1, n - 4, turn)
                if (g - V_LAG) % 2 == 0 and is_pair(g - V_LAG):
                    attend(g - V_LAG, turn)
                if (g - O_LAG) % 2 == 0 and is_pair(g - O_LAG):
                    project_out(g - O_LAG, turn)
                if n == 2 and is_row(b - 1):
                    leaves_out(b - 1, turn)
                if n == SUM_SLOT and is_row(b - 1):
                    transpose_out(b - 1, turn)

            run(pe, slot)

        @block.vector
        def _(dve):
            V = nc.vector

            V.memset(rt[:, NODES:LEAVES], 0.0)
            V.memset(ones[:], 1.0).then_inc(const_set, 1)
            dve.wait_ge(loaded_qk, LOADS_QK)
            V.tensor_tensor(bqbk[:], bqt[:], bkt[:], ALU.mult).then_inc(bqbk_made, 1)
            for n, b in enumerate(a_banks):
                h = slice(AH * n, AH * n + AH)
                dve.wait_ge(a_made, n + 1)
                V.tensor_copy(a_f[:, h, :].rearrange("p h m -> p (h m)"), b[:]).then_inc(a_kept, 1)
                dve.wait_ge(a_kept, n + 1)
                V.tensor_copy(a_hi[:, h, :], a_f[:, h, :]).then_inc(setup_copied, 1)
                dve.wait_ge(setup_copied, n + 1)
                V.tensor_tensor(a_lo[:, h, :], a_f[:, h, :], a_hi[:, h, :].bitcast(f32), ALU.subtract)
            dve.wait_ge(small_made, 1)
            V.tensor_copy(qbias[:], ps_o[:, 0:HEADS])
            for t in range(QT):
                V.tensor_copy(bqbk_sum[:, t, :], ps_o[:, 2 * HEADS:3 * HEADS])
            V.tensor_copy(kbias_f[:], ps_o[:, HEADS:2 * HEADS]).then_inc(setup_copied, 1)
            dve.wait_ge(loaded_rest, LOADS_REST)
            V.tensor_tensor(out_bias[:], bo_b[:], wb_b[:], ALU.add)
            V.tensor_copy(wv_hi[:], wv_f[:]).then_inc(setup_copied, 1)
            dve.wait_ge(setup_copied, 6)
            V.tensor_tensor(wv_lo[:], wv_f[:], wv_hi[:].bitcast(f32), ALU.subtract)
            dve.wait_ge(setup_act, 1)
            V.tensor_copy(rw_hi[:], rw_f[:]).then_inc(setup_copied, 1)
            dve.wait_ge(setup_copied, 7)
            V.tensor_tensor(rw_lo[:], rw_f[:], rw_hi[:].bitcast(f32), ALU.subtract).then_inc(setup_dve, 1)
            V.tensor_copy(wo_hi[:], wo_f[:]).then_inc(setup_copied, 1)
            dve.wait_ge(setup_copied, 8)
            V.tensor_tensor(wo_lo[:], wo_f[:], wo_hi[:].bitcast(f32), ALU.subtract).then_inc(wo_made, 1)
            dve.wait_ge(mask_made, 1)

            def keep_transposed(g, turn):
                wait(dve, pt_done[0], g + 1, turn, LOOP)
                wait(dve, pv_done, g // 2 - 1, turn, LOOP // 2)
                V.tensor_copy(pt_sb[g % PBUF][:, 0, :], ps_p[0][:, 0:BLOCKS]).then_inc(pt_kept[0], 1)

            def invert_totals(g, turn):
                wait(dve, exp_done[0], g + 1, turn, LOOP)
                wait(dve, exp_done[1], g + 1, turn, LOOP)
                wait(dve, p_scaled, g - 1, turn, LOOP)
                V.reciprocal(inv[g % 2][:], total[g % 2][:]).then_inc(inv_made, 1)

            def mask_and_shift(g, turn):
                b, n, i = g // PAIRS, g % PAIRS, g % 2
                wait(dve, exp_done[1], g - 1, turn, LOOP)
                if n == 0:
                    wait(dve, row_scaled, 2 * b + 2, turn, 4)

                def mask_rows(h, t):
                    lo, hi = ((0, P), (P, BLOCKS))[t]
                    return V.tensor_tensor_reduce(ps_s[h][:, lo:hi], ps_s[h][:, lo:hi], mask[:, lo:hi],
                                                  1.0, MASKED, ALU.add, ALU.max, top[i][:, h, t:t + 1])

                def take_shift(h):
                    dve.wait_ge(top_made, count(2 * g + h + 1, turn, 2 * LOOP))
                    V.scalar_tensor_tensor(shift[i][:, h, :], top[i][:, h, :], -SCALE,
                                           row_d[b % 2][:, :, 2 * n + h], ALU.mult, ALU.add)\
                        .then_inc(shift_made, 1)

                wait(dve, s_done[0], g + 1, turn, LOOP)
                dve.sem_inc(waits_over, 1)
                mask_rows(0, 0)
                mask_rows(0, 1).then_inc(top_made, 1)
                wait(dve, s_done[1], g + 1, turn, LOOP)
                dve.sem_inc(waits_over, 1)
                mask_rows(1, 0)
                take_shift(0)
                mask_rows(1, 1).then_inc(top_made, 1)
                if is_pair(g + 1):
                    split_projected(g + 1, turn)
                take_shift(1)

            def round_projected(g, turn):
                i = g % 2
                wait(dve, t_kept, g + 1, turn, LOOP)
                wait(dve, s_done[1], g - 1, turn, LOOP)
                V.tensor_copy(t_hi[i][:], t_sb[i][:, :, P:SEQ]).then_inc(t_rounded, 1)

            def split_projected(g, turn):
                i = g % 2
                wait(dve, t_rounded, g + 1, turn, LOOP)
                V.tensor_tensor(t_lo[i][:], t_sb[i][:, :, P:SEQ], t_hi[i][:].bitcast(f32), ALU.subtract)\
                    .then_inc(t_split, 1)

            def row_stats(b, turn):
                wait(dve, x_in[b % 2], 16 * (b // 2 + 1), turn, 16)
                wait(dve, xn_made, b, turn, 2)
                for t in range(QT):
                    last = V.bn_stats(stats[:, t, :], xin[b % 2][:, t, :])
                last.then_inc(half_stats, 1)
                wait(dve, half_stats, b + 1, turn, 2)
                dve.sem_inc(waits_over, 1)
                for t in range(QT):
                    last = V.bn_aggr(mv[:, t, :], stats[:, t, :])
                last.then_inc(stats_made, 1)

            def normalize(b, turn):
                wait(dve, rstd_made, b + 1, turn, 2)
                wait(dve, stats_made, b + 1, turn, 2)
                wait(dve, xt_done, b, turn, 2)
                for t in range(QT):
                    last = V.tensor_scalar(xn[:, t, :], xin[b % 2][:, t, :], mv[:, t, 0:1], rstd[:, t:t + 1],
                                           ALU.subtract, ALU.mult)
                last.then_inc(xn_made, 1)

            def keep_xt(b, turn):
                i = b % 2
                wait(dve, xt_done, b + 1, turn, 2)
                wait(dve, s_done[1], PAIRS * (b - 1), turn, LOOP)
                V.tensor_copy(xt_f[i][:], ps_x[:, 0:SEQ]).then_inc(xt_kept, 1)
                wait(dve, xt_kept, 2 * b + 1, turn, 4)
                V.tensor_copy(xt_hi[i][:], xt_f[i][:]).then_inc(xt_kept, 1)
                wait(dve, xt_kept, 2 * b + 2, turn, 4)
                V.tensor_tensor(xt_lo[i][:], xt_f[i][:], xt_hi[i][:].bitcast(f32), ALU.subtract)\
                    .then_inc(xt_split, 1)

            def keep_row_bias(b, turn):
                i = b % 2
                wait(dve, row_done, b + 1, turn, 2)
                if b >= 2:
                    wait(dve, shift_made, 2 * PAIRS * (b - 1), turn, 2 * LOOP)
                V.tensor_tensor(row_b[:], ps_x[:, 0:QT * HEADS].rearrange("p (t h) -> p t h", t=QT),
                                bqbk_sum[:], ALU.add).then_inc(row_kept, 1)
                wait(dve, row_kept, b + 1, turn, 2)
                V.tensor_scalar(row_bs[:], row_b[:], SCALE, None, ALU.mult).then_inc(row_scaled, 1)
                wait(dve, row_scaled, 2 * b + 1, turn, 4)
                V.scalar_tensor_tensor(row_d[i][:], row_b[:], -SCALE, row_bs[:], ALU.mult, ALU.add)\
                    .then_inc(row_scaled, 1)

            def keep_values(b, j, turn):
                t, c = j // (E // VH), j % (E // VH)
                wait(dve, v_done, VQ * b + j + 1, turn, 2 * VQ)
                wait(dve, pv_done, TWOS * (b - 1), turn, 2 * TWOS)
                V.tensor_tensor(v_sb[b % 2][:, t, c * VH:(c + 1) * VH], ps_x[:], bv_b[:, c * VH:(c + 1) * VH],
                                ALU.add).then_inc(v_kept, 1)

            def split_attended(g, turn):
                i = g // 2 % 2
                wait(dve, at_rounded, g // 2 + 1, turn, LOOP // 2)
                wait(dve, wo_done, g // 2 - 1, turn, LOOP // 2)
                V.tensor_tensor(at_lo[i][:].rearrange("p j q -> p (j q)"), ps_o[:],
                                at_hi[i][:].bitcast(f32).rearrange("p j q -> p (j q)"), ALU.subtract)\
                    .then_inc(at_split, 1)

            def finish(b, turn):
                wait(dve, out_done, b + 1, turn, 2)
                wait(dve, res_made, b + 1, turn, 2)
                r = res[b % 2][:].rearrange("p t m -> p (t m)")
                V.tensor_tensor(r, ps_w[:, 0:QT * DM], r, ALU.add).then_inc(out_made, 1)

            def slot(g, turn):
                b, n = g // PAIRS, g % PAIRS
                if is_pair(g - 1):
                    invert_totals(g - 1, turn)
                if is_pair(g + 1):
                    round_projected(g + 1, turn)
                if n == SUM_SLOT + 1 and is_row(b - 1):
                    finish(b - 1, turn)
                if is_pair(g):
                    mask_and_shift(g, turn)
                elif is_pair(g + 1):
                    split_projected(g + 1, turn)
                if (g - O_LAG) % 2 == 0 and is_pair(g - O_LAG):
                    split_attended(g - O_LAG, turn)
                if is_pair(g - T_LAG):
                    keep_transposed(g - T_LAG, turn)
                if n == 0 and is_row(b + 1):
                    row_stats(b + 1, turn)
                if n == 1 and is_row(b + 1):
                    normalize(b + 1, turn)
                if n == 2 and is_row(b + 1):
                    keep_xt(b + 1, turn)
                if n == 3 and is_row(b + 1):
                    keep_row_bias(b + 1, turn)
                if n >= 4 and is_row(b + 1):
                    keep_values(b + 1, n - 4, turn)

            run(dve, slot)

        @block.scalar
        def _(act):
            A = nc.scalar

            act.wait_ge(rw_made, 1)
            A.activation(rw_f[:], ps_x[:, 0:LEAVES], ACT.Copy).then_inc(setup_act, 1)
            act.wait_ge(lw_made, 1)
            A.activation(lw[:].rearrange("p c m -> p (c m)"), ps_t[:, 0:LC * DM], ACT.Copy,
                         scale=float(0.5 ** DEPTH)).then_inc(lw_kept, 1)
            act.wait_ge(setup_copied, 5)

            def keep_transposed(g, h, turn):
                wait(act, pt_done[h], g + 1, turn, LOOP)
                wait(act, pv_done, g // 2 - 1, turn, LOOP // 2)
                A.activation(pt_sb[g % PBUF][:, h, :], ps_p[h][:, 0:BLOCKS], ACT.Copy).then_inc(pt_kept[h], 1)

            def exponentials(g, turn):
                i = g % 2
                wait(act, pt_done[1], g - PBUF + 1, turn, LOOP)
                wait(act, inv_made, g - 1, turn, LOOP)
                for h in range(2):
                    act.wait_ge(shift_made, count(2 * g + h + 1, turn, 2 * LOOP))
                    for t, (lo, hi) in enumerate(((0, P), (P, BLOCKS))):
                        last = A.activation(p_sb[g % PBUF][:, h, lo:hi], ps_s[h][:, lo:hi], ACT.Exp,
                                            bias=shift[i][:, h, t:t + 1], scale=SCALE,
                                            accum_out=total[i][:, h, t:t + 1])
                    last.then_inc(exp_done[h], 1)

            def keep_projected(g, turn):
                n = g % PAIRS
                wait(act, t_done, g + 1, turn, LOOP)
                wait(act, s_done[1], g - 1, turn, LOOP)
                for h in range(2):
                    last = A.activation(t_sb[g % 2][:, h, :], ps_t[:, h * SEQ:(h + 1) * SEQ], ACT.Identity,
                                        bias=qbias[:, 2 * n + h:2 * n + h + 1])
                last.then_inc(t_kept, 1)

            def round_attended(g, turn):
                wait(act, pv_done, g // 2 + 1, turn, LOOP // 2)
                wait(act, wo_done, g // 2 - 1, turn, LOOP // 2)
                A.activation(at_hi[g // 2 % 2][:].rearrange("p j q -> p (j q)"), ps_o[:], ACT.Copy)\
                    .then_inc(at_rounded, 1)

            def keep_sum(b, turn):
                wait(act, wo_done, TWOS * (b + 1), turn, 2 * TWOS)
                wait(act, out_done, b, turn, 2)
                A.activation(sum_t[:], ps_w[:, 0:SEQ], ACT.Copy).then_inc(sum_kept, 1)

            def gates(b, turn):
                wait(act, logits_done, b + 1, turn, 2)
                wait(act, branch_made, b, turn, 2)
                A.activation(th[:].rearrange("p t n -> p (t n)"), ps_x[:], ACT.Tanh, scale=0.5)\
                    .then_inc(tanh_made, 1)

            def keep_leaves(b, turn):
                wait(act, leaft_done, b + 1, turn, 2)
                wait(act, leaves_done, b, turn, 2)
                A.activation(leaf_t[:].rearrange("p c q -> p (c q)"), ps_x[:], ACT.Copy).then_inc(leaft_kept, 1)

            def slot(g, turn):
                b, n = g // PAIRS, g % PAIRS
                if n == SUM_SLOT and is_row(b - 1):
                    keep_sum(b - 1, turn)
                if is_pair(g):
                    exponentials(g, turn)
                if is_pair(g + 2):
                    keep_projected(g + 2, turn)
                if is_pair(g - T_LAG):
                    keep_transposed(g - T_LAG, 1, turn)
                if (g - V_LAG) % 2 == 0 and is_pair(g - V_LAG):
                    round_attended(g - V_LAG, turn)
                if n == 0 and is_row(b):
                    gates(b, turn)
                if n == 1 and is_row(b - 1):
                    keep_leaves(b - 1, turn)

            run(act, slot)

        @block.gpsimd
        def _(pool):
            G = nc.gpsimd

            G.memset(ident[:], 0.0)
            G.memset(minus_half[:], -0.5)
            G.memset(eps[:], EPS)
            G.memset(mask[:], 0.0).then_inc(const_set, 1)
            pool.wait_ge(const_set, 2)
            G.affine_select(out=ident[:], in_=ident[:], compare_op=ALU.not_equal, fill=1.0, base=0,
                            pattern=[[-1, P]], channel_multiplier=1).then_inc(ident_made, 1)
            G.affine_select(out=mask[:, 0:P], in_=mask[:, 0:P], compare_op=ALU.is_ge, fill=MASKED, base=0,
                            pattern=[[-1, P]], channel_multiplier=1)
            G.affine_select(out=mask[:, 2 * P:3 * P], in_=mask[:, 2 * P:3 * P], compare_op=ALU.is_ge,
                            fill=MASKED, base=0, pattern=[[-1, P]], channel_multiplier=1).then_inc(mask_made, 1)
            pool.wait_ge(setup_dve, 1)

            def scale_probabilities(g, turn):
                wait(pool, inv_made, g + 1, turn, LOOP)
                p, r = p_sb[g % PBUF], inv[g % 2]
                for t, (lo, hi) in enumerate(((0, P), (P, BLOCKS))):
                    last = G.tensor_tensor(p[:, :, lo:hi], p[:, :, lo:hi],
                                           r[:, :, t:t + 1].to_broadcast([P, 2, hi - lo]), ALU.mult)
                last.then_inc(p_scaled, 1)

            def reciprocal_deviation(b, turn):
                wait(pool, stats_made, b + 1, turn, 2)
                wait(pool, xn_made, b, turn, 2)
                G.tensor_tensor(var_eps[:], mv[:, :, 1], eps[:], ALU.add).then_inc(var_made, 1)
                wait(pool, var_made, b + 1, turn, 2)
                G.tensor_tensor(rstd[:], var_eps[:], minus_half[:], ALU.pow).then_inc(rstd_made, 1)

            def branches(b, turn):
                wait(pool, tanh_made, b + 1, turn, 2)
                one = ones[:, 0:1, None].to_broadcast([P, QT, LEAVES])
                G.tensor_tensor(branch[:, :, :, 0], one, th[:], ALU.subtract)
                G.tensor_tensor(branch[:, :, :, 1], one, th[:], ALU.add).then_inc(branch_made, 1)

            def tree_levels(b, levels, turn):
                for level in levels:
                    n = 2 ** level
                    if level == 1:
                        wait(pool, branch_made, b + 1, turn, 2)
                        parent = branch[:, :, 0, :]
                        wait(pool, leaft_done, b, turn, 2)
                    else:
                        parent = prob[level % 2][:, :, 0:n]
                        pool.wait_ge(level_made, count((DEPTH - 2) * b + level - 1, turn, 2 * (DEPTH - 2)))
                    last = G.tensor_tensor(
                        prob[(level + 1) % 2][:, :, 0:2 * n].rearrange("p t (n c) -> p t n c", c=2),
                        parent[:, :, :, None].to_broadcast([P, QT, n, 2]),
                        branch[:, :, n - 1:2 * n - 1, :], ALU.mult)
                    if level < DEPTH - 1:
                        last.then_inc(level_made, 1)
                    else:
                        last.then_inc(leaf_made, 1)

            def residual(b, turn):
                wait(pool, x_in[b % 2], 16 * (b // 2 + 1), turn, 16)
                wait(pool, xn_made, b + 1, turn, 2)
                wait(pool, stored[b % 2], 16 * (b // 2), turn, 16)
                G.tensor_tensor(res[b % 2][:], xin[b % 2][:],
                                out_bias[:, None, :].to_broadcast([P, QT, DM]), ALU.add).then_inc(res_made, 1)

            def slot(g, turn):
                b, n = g // PAIRS, g % PAIRS
                if is_pair(g - 1):
                    scale_probabilities(g - 1, turn)
                if n == 0 and is_row(b + 1):
                    reciprocal_deviation(b + 1, turn)
                if n == 1 and is_row(b):
                    branches(b, turn)
                if n == 2 and is_row(b):
                    tree_levels(b, range(1, 5), turn)
                if n == 3 and is_row(b):
                    tree_levels(b, range(5, DEPTH), turn)
                if n == 7 and is_row(b + 1):
                    residual(b + 1, turn)

            run(pool, slot)


def kernel(**inputs):
    import numpy as np
    import concourse.bacc as bacc
    from concourse.bass_utils import run_bass_kernel_spmd

    def given(name):
        return np.asarray(inputs[name])

    laid_out = {
        "x": given("L0_attn_residual"),
        "wq_t": given("L0_attn_W_Q").transpose(2, 0, 1),
        "wk_t": given("L0_attn_W_K").transpose(2, 0, 1),
        "wv": given("L0_attn_W_V"),
        "wo": given("L0_attn_W_O"),
        "bq_t": given("L0_attn_b_Q").T,
        "bk_t": given("L0_attn_b_K").T,
        "bv": given("L0_attn_b_V"),
        "bo": given("L0_attn_b_O"),
        "ffn_wq": given("L0_ffn_Wq"),
        "routers_t": given("L0_ffn_routers").T,
        "leaf_values_t": given("L0_ffn_leaf_values").T,
        "wout_t": given("L0_ffn_Wout_w").T,
        "wout_b": given("L0_ffn_Wout_b"),
    }
    nc = bacc.Bacc("TRN2", target_bir_lowering=False, num_devices=1)
    arrays, args = {}, []
    for name, a in laid_out.items():
        a = np.ascontiguousarray(a)
        arrays[f"in_{name}"] = a
        args.append(nc.dram_tensor(f"in_{name}", a.shape, mybir.dt.from_np(a.dtype), kind="ExternalInput").ap())
    out = nc.dram_tensor("out", laid_out["x"].shape, mybir.dt.float32, kind="ExternalOutput").ap()
    attention_and_tree_ffn(nc, *args, out)
    result = run_bass_kernel_spmd(nc, [arrays], core_ids=[0])
    return result.results[0]["out"]
```

```python
import concourse.bass as bass
from concourse import mybir
from contextlib import ExitStack


def attention_and_tree_ffn(nc, x, wq_t, wk_t, wv, wo, bq_t, bk_t, bv, bo, ffn_wq, routers_t,
                           leaf_values_t, wout_t, wout_b, out):
    f32 = mybir.dt.float32
    f32r = mybir.dt.float32r
    ALU = mybir.AluOpType
    ACT = mybir.ActivationFunctionType

    BATCH, SEQ, DM = x.shape
    HEADS, _, DH = wv.shape
    P = 128
    QT = SEQ // P
    PAIRS = HEADS // 2
    E = HEADS * DH
    NODES = routers_t.shape[1]
    LEAVES = NODES + 1
    DEPTH = LEAVES.bit_length() - 1
    LC = LEAVES // P
    SCALE = float(DH) ** -0.5
    EPS = 1e-5
    BLOCKS = 3 * P
    MASKED = -3.0e38
    VH = 512
    VQ = QT * E // VH
    PBUF = 4

    SLOTS = BATCH * PAIRS
    LOOP = 2 * PAIRS
    FIRST, START = -2, PAIRS
    TURNS = (SLOTS - START) // LOOP
    END = START + TURNS * LOOP
    T_LAG, V_LAG, O_LAG = 2, 4, 5
    SUM_SLOT = O_LAG - 1
    LAST = SLOTS + SUM_SLOT + 1
    TWOS = PAIRS // 2

    x_v = x.rearrange("b (t p) m -> b p t m", p=P)
    out_v = out.rearrange("b (t p) m -> b p t m", p=P)

    with ExitStack() as ctx:
        def sb(name, shape, dt=f32):
            return ctx.enter_context(nc.sbuf_tensor(name, shape, dt))

        def bank(name):
            return ctx.enter_context(nc.psum_tensor(name, [P, 512], f32))

        def sem(name):
            return ctx.enter_context(nc.semaphore(name))

        wqt = sb("wqt", [P, PAIRS, DM])
        wkt = sb("wkt", [P, PAIRS, DM])
        wv_f = sb("wv_f", [DM, E])
        wo_f = sb("wo_f", [P, PAIRS, DM])
        bqt = sb("bqt", [P, PAIRS])
        bkt = sb("bkt", [P, PAIRS])
        bv_b = sb("bv_b", [P, E])
        bo_b = sb("bo_b", [P, DM])
        wb_b = sb("wb_b", [P, DM])
        fwq = sb("fwq", [DM, DM])
        rt = sb("rt", [DM, LEAVES])
        lvt = sb("lvt", [DM, LEAVES])
        wot = sb("wot", [DM, DM])
        a_hi = sb("a_hi", [DM, HEADS, DM], f32r)
        a_lo = sb("a_lo", [DM, HEADS, DM], f32r)
        wv_hi = sb("wv_hi", [DM, E], f32r)
        wv_lo = sb("wv_lo", [DM, E], f32r)
        rw_hi = sb("rw_hi", [DM, LEAVES], f32r)
        rw_lo = sb("rw_lo", [DM, LEAVES], f32r)
        wo_hi = sb("wo_hi", [P, PAIRS, DM], f32r)
        wo_lo = sb("wo_lo", [P, PAIRS, DM], f32r)
        lw = sb("lw", [P, LC, DM])
        lw_hi = sb("lw_hi", [P, LC, DM], f32r)
        lw_lo = sb("lw_lo", [P, LC, DM], f32r)
        query_bias = sb("query_bias", [DM, HEADS])
        key_bias = sb("key_bias", [DM, HEADS])
        by_head = sb("by_head", [P, 3, PAIRS, 2])
        bqbk_sum = sb("bqbk_sum", [P, QT, HEADS])
        out_bias = sb("out_bias", [P, DM])
        ident = sb("ident", [P, P])
        ones = sb("ones", [P, P])
        mask = sb("mask", [P, BLOCKS])
        xin = [sb(f"xin{i}", [P, QT, DM]) for i in range(2)]
        res = [sb(f"res{i}", [P, QT, DM]) for i in range(2)]
        stats = sb("stats", [P, QT, 6])
        mv = sb("mv", [P, QT, 2])
        var_eps = sb("var_eps", [P, QT])
        minus_half = sb("minus_half", [P, QT])
        eps = sb("eps", [P, QT])
        rstd = sb("rstd", [P, QT])
        xn = sb("xn", [P, QT, DM])
        xt_f = [sb(f"xt_f{i}", [DM, SEQ]) for i in range(2)]
        xt_hi = [sb(f"xt_hi{i}", [DM, SEQ], f32r) for i in range(2)]
        xt_lo = [sb(f"xt_lo{i}", [DM, SEQ], f32r) for i in range(2)]
        row_b = sb("row_b", [P, QT, HEADS])
        row_bs = sb("row_bs", [P, QT, HEADS])
        row_d = [sb(f"row_d{i}", [P, QT, HEADS]) for i in range(2)]
        v_sb = [sb(f"v_sb{i}", [P, QT, E]) for i in range(2)]
        th = sb("th", [P, QT, LEAVES])
        branch = sb("branch", [P, QT, LEAVES, 2])
        prob = [sb(f"prob{i}", [P, QT, LEAVES]) for i in range(2)]
        leaf_t = sb("leaf_t", [P, LC, SEQ])
        leaf_hi = sb("leaf_hi", [P, LC, SEQ], f32r)
        leaf_lo = sb("leaf_lo", [P, LC, SEQ], f32r)
        sum_t = sb("sum_t", [DM, SEQ])
        t_sb = [sb(f"t_sb{i}", [DM, 2, SEQ]) for i in range(2)]
        t_hi = [sb(f"t_hi{i}", [DM, 2, P], f32r) for i in range(2)]
        t_lo = [sb(f"t_lo{i}", [DM, 2, P], f32r) for i in range(2)]
        top = [sb(f"top{i}", [P, 2, QT]) for i in range(2)]
        shift = [sb(f"shift{i}", [P, 2, QT]) for i in range(2)]
        total = [sb(f"total{i}", [P, 2, QT]) for i in range(2)]
        inv = [sb(f"inv{i}", [P, 2, QT]) for i in range(2)]
        p_sb = [sb(f"p_sb{i}", [P, 2, BLOCKS]) for i in range(PBUF)]
        pt_sb = [sb(f"pt_sb{i}", [P, 2, BLOCKS]) for i in range(PBUF)]
        at_hi = [sb(f"at_hi{i}", [P, 2, SEQ], f32r) for i in range(2)]
        at_lo = [sb(f"at_lo{i}", [P, 2, SEQ], f32r) for i in range(2)]

        ps_s = [bank("ps_s0"), bank("ps_s1")]
        ps_p = [bank("ps_p0"), bank("ps_p1")]
        ps_t = bank("ps_t")
        ps_o = bank("ps_o")
        ps_w = bank("ps_w")
        ps_x = bank("ps_x")

        loaded_qk = [sem("loaded_qk0"), sem("loaded_qk1")]
        loaded_biases = sem("loaded_biases")
        loaded_ffn = sem("loaded_ffn")
        loaded_v = sem("loaded_v")
        loaded_leaves = sem("loaded_leaves")
        loaded_out = sem("loaded_out")
        const_set = sem("const_set")
        zeros_set = sem("zeros_set")
        ident_made = sem("ident_made")
        mask_made = sem("mask_made")
        by_head_made = sem("by_head_made")
        a_made = sem("a_made")
        a_rounded = sem("a_rounded")
        a_split = sem("a_split")
        biases_made = sem("biases_made")
        biases_kept = sem("biases_kept")
        rw_made = sem("rw_made")
        rw_rounded = sem("rw_rounded")
        rw_split = sem("rw_split")
        wv_rounded = sem("wv_rounded")
        wv_split = sem("wv_split")
        wo_rounded = sem("wo_rounded")
        wo_split = sem("wo_split")
        lw_made = sem("lw_made")
        lw_kept = sem("lw_kept")
        lw_rounded = sem("lw_rounded")
        lw_split = sem("lw_split")
        out_bias_made = sem("out_bias_made")
        waits_over = sem("waits_over")
        x_in = [sem("x_in0"), sem("x_in1")]
        stored = [sem("stored0"), sem("stored1")]
        bn_stats_made = sem("bn_stats_made")
        stats_made = sem("stats_made")
        var_made = sem("var_made")
        rstd_made = sem("rstd_made")
        xn_made = sem("xn_made")
        res_made = sem("res_made")
        xt_done = sem("xt_done")
        xt_kept = sem("xt_kept")
        xt_split = sem("xt_split")
        row_done = sem("row_done")
        row_kept = sem("row_kept")
        row_scaled = sem("row_scaled")
        v_done = sem("v_done")
        v_kept = sem("v_kept")
        logits_done = sem("logits_done")
        tanh_made = sem("tanh_made")
        branch_made = sem("branch_made")
        level_made = sem("level_made")
        leaf_made = sem("leaf_made")
        leaft_done = sem("leaft_done")
        leaft_kept = sem("leaft_kept")
        leaft_rounded = sem("leaft_rounded")
        leaft_split = sem("leaft_split")
        leaves_done = sem("leaves_done")
        sum_kept = sem("sum_kept")
        out_done = sem("out_done")
        out_made = sem("out_made")
        t_done = sem("t_done")
        t_kept = sem("t_kept")
        t_rounded = sem("t_rounded")
        t_split = sem("t_split")
        s_done = [sem("s_done0"), sem("s_done1")]
        top_made = sem("top_made")
        shift_made = sem("shift_made")
        exp_done = [sem("exp_done0"), sem("exp_done1")]
        inv_made = sem("inv_made")
        p_scaled = sem("p_scaled")
        pt_done = [sem("pt_done0"), sem("pt_done1")]
        pt_kept = [sem("pt_kept0"), sem("pt_kept1")]
        pv_done = sem("pv_done")
        at_rounded = sem("at_rounded")
        at_split = sem("at_split")
        wo_done = sem("wo_done")

        def count(n, turn, per_turn):
            return n if turn is None else turn * per_turn + n

        def wait(eng, s, n, turn, per_turn):
            if n > 0:
                eng.wait_ge(s, count(n, turn, per_turn))

        def run(eng, slot):
            for g in range(FIRST, START):
                slot(g, None)
            with eng.Fori(0, TURNS) as turn:
                for g in range(START, START + LOOP):
                    slot(g, turn)
            for g in range(END, LAST + 1):
                slot(g, None)

        def is_pair(g):
            return 0 <= g < SLOTS

        def is_row(b):
            return 0 <= b < BATCH

        block = ctx.enter_context(nc.Block())

        @block.sync
        def _(sp):
            def load(dst, src, s):
                sp.dma_start(dst, src).then_inc(s, 16)

            def load_x(b, turn):
                wait(sp, res_made, b - 1, turn, 2)
                row = b if turn is None else turn * 2 + b
                sp.dma_start(xin[b % 2][:], x_v[bass.ds(row, 1)].rearrange("b p t m -> (b p) t m"))\
                    .then_inc(x_in[b % 2], 16)

            def store(b, turn):
                wait(sp, out_made, b + 1, turn, 2)
                row = b if turn is None else turn * 2 + b
                sp.dma_start(out_v[bass.ds(row, 1)].rearrange("b p t m -> (b p) t m"), res[b % 2][:])\
                    .then_inc(stored[b % 2], 16)

            load_x(0, None)
            for i in range(2):
                half = slice(i * PAIRS // 2, (i + 1) * PAIRS // 2)
                load(wqt[:, half, :], wq_t[:, half, :], loaded_qk[i])
                load(wkt[:, half, :], wk_t[:, half, :], loaded_qk[i])
                if i == 0:
                    load(bqt[:], bq_t, loaded_biases)
                    load(bkt[:], bk_t, loaded_biases)
            load(fwq[:], ffn_wq, loaded_ffn)
            load(rt[:, 0:NODES], routers_t, loaded_ffn)
            load(wv_f[:].rearrange("m (h d) -> m h d", h=HEADS), wv.rearrange("h m d -> m h d"), loaded_v)
            load(bv_b[:], bv.rearrange("h d -> (h d)")[None, :].to_broadcast([P, E]), loaded_v)
            load_x(1, None)
            load(lvt[:], leaf_values_t, loaded_leaves)
            load(wot[:], wout_t, loaded_leaves)
            load(wo_f[:], wo.rearrange("(c p) m -> p c m", p=P), loaded_out)
            load(bo_b[:], bo[None, :].to_broadcast([P, DM]), loaded_out)
            load(wb_b[:], wout_b[None, :].to_broadcast([P, DM]), loaded_out)
            load_x(2, None)
            turns = (BATCH - 4) // 2
            with sp.Fori(0, turns) as turn:
                for b in range(2):
                    load_x(b + 3, turn)
                    store(b, turn)
            for b in range(2 * turns, BATCH):
                if b + 3 < BATCH:
                    load_x(b + 3, None)
                store(b, None)
            for i in range(2):
                sp.wait_ge(stored[i], 16 * BATCH // 2)

        a_banks = [ps_s[0], ps_s[1], ps_p[0], ps_p[1]]
        AH = 512 // DM

        def a_heads(n):
            first = n // 2 * 2 * AH + n % 2
            return slice(first, first + 2 * AH - 1, 2)

        def v_bank(b):
            return ps_w if b == 0 else ps_x

        @block.tensor
        def _(pe):
            def split_product(dst, lhs_hi, lhs_lo, rhs_hi, rhs_lo):
                nc.tensor.matmul(dst, lhs_hi, rhs_hi, start=True, stop=False)
                nc.tensor.matmul(dst, lhs_hi, rhs_lo, start=False, stop=False)
                return nc.tensor.matmul(dst, lhs_lo, rhs_hi, start=False, stop=True)

            def make_a(i):
                pe.wait_ge(loaded_qk[i], 2 * 16)
                for k in range(AH):
                    for odd in range(2):
                        d, n = slice(odd * DH, (odd + 1) * DH), AH * i + k
                        last = nc.tensor.matmul(a_banks[2 * i + odd][:, k * DM:(k + 1) * DM],
                                                wqt[d, n, :], wkt[d, n, :], start=True, stop=True)
                        if k == AH - 1:
                            last.then_inc(a_made, 1)

            def make_query_bias():
                pe.wait_ge(by_head_made, 1)
                pe.wait_ge(loaded_qk[1], 2 * 16)
                for n in range(PAIRS):
                    last = nc.tensor.matmul(ps_o[:, 2 * n:2 * n + 2], wkt[:, n, :], by_head[:, 0, n, :],
                                            start=True, stop=True)
                last.then_inc(biases_made, 1)

            def make_key_bias():
                pe.wait_ge(biases_kept, 1)
                for n in range(PAIRS):
                    nc.tensor.matmul(ps_o[:, 2 * n:2 * n + 2], wqt[:, n, :], by_head[:, 1, n, :],
                                     start=True, stop=True)
                nc.tensor.matmul(ps_o[:, HEADS:2 * HEADS], ones[:],
                                 by_head[:, 2, :, :].rearrange("p n h -> p (n h)"), start=True, stop=True)\
                    .then_inc(biases_made, 1)

            def make_rw():
                pe.wait_ge(const_set, 2)
                pe.wait_ge(loaded_ffn, 2 * 16)
                nc.tensor.matmul(ps_w[:, 0:LEAVES], fwq[:], rt[:], start=True, stop=True).then_inc(rw_made, 1)

            def make_lw():
                pe.wait_ge(loaded_leaves, 2 * 16)
                pe.wait_ge(tanh_made, 1)
                for c in range(LC):
                    last = nc.tensor.matmul(ps_x[:, c * DM:(c + 1) * DM], lvt[:, c * P:(c + 1) * P], wot[:],
                                            start=True, stop=True)
                last.then_inc(lw_made, 1)

            def transpose_probabilities(g, turn):
                wait(pe, p_scaled, g + 1, turn, LOOP)
                for h in range(2):
                    wait(pe, pt_kept[h], g, turn, LOOP)
                    for n in range(BLOCKS // P):
                        last = nc.tensor.transpose(ps_p[h][:, n * P:(n + 1) * P],
                                                   p_sb[g % PBUF][:, h, n * P:(n + 1) * P], ident[:])
                    last.then_inc(pt_done[h], 1)

            def scores(g, turn):
                wait(pe, t_split, g + 1, turn, LOOP)
                i, b = g % 2, g // PAIRS % 2
                for h in range(2):
                    wait(pe, exp_done[h], g, turn, LOOP)
                    nc.tensor.matmul(ps_s[h][:, 0:P], t_sb[i][:, h, 0:P], xt_f[b][:, 0:P], start=True, stop=True)
                    split_product(ps_s[h][:, P:BLOCKS], t_hi[i][:, h, :], t_lo[i][:, h, :],
                                  xt_hi[b][:], xt_lo[b][:]).then_inc(s_done[h], 1)

            def project(g, turn):
                b, n = g // PAIRS, g % PAIRS
                if n == 0:
                    wait(pe, xt_split, b + 1, turn, 2)
                if b == 0 and n % AH == 0:
                    pe.wait_ge(a_split, 2 * (n // AH + 1))
                wait(pe, t_kept, g, turn, LOOP)
                for h in range(2):
                    last = split_product(ps_t[:, h * SEQ:(h + 1) * SEQ],
                                         a_hi[:, 2 * n + h, :], a_lo[:, 2 * n + h, :],
                                         xt_hi[b % 2][:], xt_lo[b % 2][:])
                last.then_inc(t_done, 1)

            def attend(g, turn):
                b, n = g // PAIRS, g % PAIRS
                if n == 0:
                    wait(pe, v_kept, VQ * (b + 1), turn, 2 * VQ)
                for h in range(2):
                    wait(pe, pt_kept[h], g + 2, turn, LOOP)
                wait(pe, at_split, g // 2, turn, LOOP // 2)
                for j in range(2):
                    for k, (lo, hi, q) in enumerate(((0, 2 * P, 0), (2 * P, 3 * P, P))):
                        for h in range(2):
                            col = (2 * (n + j) + h) * DH
                            last = nc.tensor.matmul(ps_o[h * DH:(h + 1) * DH, j * SEQ + q:(j + 1) * SEQ],
                                                    v_sb[b % 2][:, k, col:col + DH],
                                                    pt_sb[(g + j) % PBUF][:, h, lo:hi],
                                                    start=(j == 0 and k == 0), stop=(k == 1),
                                                    skip_group_check=True)
                last.then_inc(pv_done, 1)

            def project_out(g, turn):
                b, n, i = g // PAIRS, g % PAIRS, g // 2 % 2
                wait(pe, at_rounded, g // 2 + 1, turn, LOOP // 2)
                if g == 0:
                    pe.wait_ge(wo_split, 1)
                if n == 0:
                    wait(pe, out_made, b, turn, 2)
                for k, (w, at) in enumerate(((wo_hi, at_hi), (wo_lo, at_hi), (wo_hi, at_lo))):
                    if k == 2:
                        wait(pe, at_split, g // 2 + 1, turn, LOOP // 2)
                    for j in range(2):
                        last = nc.tensor.matmul(ps_w[:, 0:SEQ], w[:, n + j, :], at[i][:, j, :],
                                                start=(n + j == 0 and k == 0), stop=(n + j == PAIRS - 1 and k == 2),
                                                skip_group_check=True)
                last.then_inc(wo_done, 1)

            def transpose_out(b, turn):
                wait(pe, sum_kept, b + 1, turn, 2)
                for t in range(QT):
                    last = nc.tensor.transpose(ps_w[:, t * DM:(t + 1) * DM], sum_t[:, t * P:(t + 1) * P], ident[:])
                last.then_inc(out_done, 1)

            def gate_logits(b, turn):
                if b == 0:
                    pe.wait_ge(rw_split, 1)
                    pe.wait_ge(row_kept, 1)
                else:
                    wait(pe, v_kept, VQ * (b + 1), turn, 2 * VQ)
                for t in range(QT):
                    q = slice(t * P, (t + 1) * P)
                    last = split_product(ps_x[:, t * LEAVES:(t + 1) * LEAVES], xt_hi[b % 2][:, q],
                                         xt_lo[b % 2][:, q], rw_hi[:], rw_lo[:])
                last.then_inc(logits_done, 1)

            def transpose_leaves(b, turn):
                wait(pe, leaf_made, b + 1, turn, 2)
                wait(pe, tanh_made, min(b + 2, BATCH), turn, 2)
                for c in range(LC):
                    for t in range(QT):
                        last = nc.tensor.transpose(ps_x[:, c * SEQ + t * P:c * SEQ + (t + 1) * P],
                                                   prob[DEPTH % 2][:, t, c * P:(c + 1) * P], ident[:])
                last.then_inc(leaft_done, 1)

            def leaves_out(b, turn):
                if b == 0:
                    pe.wait_ge(lw_split, 1)
                wait(pe, leaft_split, b + 1, turn, 2)
                for c in range(LC):
                    for w, leaf in ((lw_hi, leaf_hi), (lw_lo, leaf_hi), (lw_hi, leaf_lo)):
                        last = nc.tensor.matmul(ps_w[:, 0:SEQ], w[:, c, :], leaf[:, c, :], start=False, stop=False,
                                                skip_group_check=True)
                last.then_inc(leaves_done, 1)

            def transpose_x(b, turn):
                wait(pe, xn_made, b + 1, turn, 2)
                wait(pe, leaft_kept, b - 1, turn, 2)
                if b == 1:
                    pe.wait_ge(lw_kept, 1)
                for t in range(QT):
                    last = nc.tensor.transpose(ps_x[:, t * P:(t + 1) * P], xn[:, t, :], ident[:])
                last.then_inc(xt_done, 1)

            def row_bias(b, turn):
                wait(pe, xt_split, b + 1, turn, 2)
                if b == 0:
                    pe.wait_ge(biases_kept, 2)
                for t in range(QT):
                    last = nc.tensor.matmul(ps_x[:, t * HEADS:(t + 1) * HEADS], xt_f[b % 2][:, t * P:(t + 1) * P],
                                            key_bias[:], start=True, stop=True)
                last.then_inc(row_done, 1)

            def values(b, j, turn):
                wait(pe, row_kept, b + 1, turn, 2)
                wait(pe, v_kept, VQ * b + j, turn, 2 * VQ)
                t, c = j // (E // VH), j % (E // VH)
                q = slice(t * P, (t + 1) * P)
                if b == 0 and j == 0:
                    pe.wait_ge(wv_split, 1)
                split_product(v_bank(b)[:], xt_hi[b % 2][:, q], xt_lo[b % 2][:, q], wv_hi[:, c * VH:(c + 1) * VH],
                              wv_lo[:, c * VH:(c + 1) * VH]).then_inc(v_done, 1)

            def slot(g, turn):
                b, n = g // PAIRS, g % PAIRS
                if is_pair(g):
                    scores(g, turn)
                if is_pair(g + 2):
                    project(g + 2, turn)
                if is_pair(g - T_LAG):
                    transpose_probabilities(g - T_LAG, turn)
                if g == FIRST:
                    make_key_bias()
                    make_rw()
                    row_bias(0, None)
                if g == 0:
                    make_a(1)
                if n == 0 and is_row(b):
                    gate_logits(b, turn)
                if n == 1 and is_row(b - 1):
                    transpose_leaves(b - 1, turn)
                if n == 2 and is_row(b + 1):
                    transpose_x(b + 1, turn)
                if n == 3 and is_row(b + 1):
                    row_bias(b + 1, turn)
                if n >= VQ and 0 < b + 1 < BATCH:
                    values(b + 1, n - VQ, turn)
                if g == 1:
                    make_lw()
                if 0 <= g < VQ:
                    values(0, g, None)
                if (g - V_LAG) % 2 == 0 and is_pair(g - V_LAG):
                    attend(g - V_LAG, turn)
                if n == 3 and is_row(b - 1):
                    leaves_out(b - 1, turn)
                if (g - O_LAG) % 2 == 0 and is_pair(g - O_LAG):
                    project_out(g - O_LAG, turn)
                if n == SUM_SLOT and is_row(b - 1):
                    transpose_out(b - 1, turn)

            make_a(0)
            pe.wait_ge(ident_made, 1)
            transpose_x(0, None)
            make_query_bias()
            run(pe, slot)

        @block.vector
        def _(dve):
            V = nc.vector

            def lay_biases_by_head():
                dve.wait_ge(zeros_set, 1)
                dve.wait_ge(loaded_biases, 2 * 16)
                for h in range(2):
                    d = slice(h * DH, (h + 1) * DH)
                    V.tensor_copy(by_head[d, 0, :, h], bqt[d, :])
                    V.tensor_copy(by_head[d, 1, :, h], bkt[d, :])
                    last = V.tensor_tensor(by_head[d, 2, :, h], bqt[d, :], bkt[d, :], ALU.mult)
                last.then_inc(by_head_made, 1)

            def split_a(n):
                h = a_heads(n)
                dve.wait_ge(a_rounded, n + 1)
                V.tensor_tensor(a_lo[:, h, :], a_banks[n][:].rearrange("p (h m) -> p h m", m=DM),
                                a_hi[:, h, :].bitcast(f32), ALU.subtract)\
                    .then_inc(a_split, 1)

            def keep_query_bias():
                dve.wait_ge(biases_made, 1)
                V.tensor_copy(query_bias[:], ps_o[:, 0:HEADS]).then_inc(biases_kept, 1)

            def keep_key_bias():
                dve.wait_ge(biases_made, 2)
                V.tensor_copy(key_bias[:], ps_o[:, 0:HEADS])
                for t in range(QT):
                    last = V.tensor_copy(bqbk_sum[:, t, :], ps_o[:, HEADS:2 * HEADS])
                last.then_inc(biases_kept, 1)

            def split_weights(hi, lo, exact, rounded, split):
                dve.wait_ge(rounded, 1)
                V.tensor_tensor(lo, exact, hi.bitcast(f32), ALU.subtract).then_inc(split, 1)

            def split_out_weights():
                split_weights(wo_hi[:], wo_lo[:], wo_f[:], wo_rounded, wo_split)
                dve.wait_ge(loaded_out, 3 * 16)
                V.tensor_tensor(out_bias[:], bo_b[:], wb_b[:], ALU.add).then_inc(out_bias_made, 1)

            def keep_transposed(g, turn):
                wait(dve, pt_done[0], g + 1, turn, LOOP)
                wait(dve, pv_done, g // 2 - 1, turn, LOOP // 2)
                V.tensor_copy(pt_sb[g % PBUF][:, 0, :], ps_p[0][:, 0:BLOCKS]).then_inc(pt_kept[0], 1)

            def invert_totals(g, turn):
                wait(dve, exp_done[0], g + 1, turn, LOOP)
                wait(dve, exp_done[1], g + 1, turn, LOOP)
                wait(dve, p_scaled, g - 1, turn, LOOP)
                V.reciprocal(inv[g % 2][:], total[g % 2][:]).then_inc(inv_made, 1)

            def mask_and_shift(g, turn):
                b, n, i = g // PAIRS, g % PAIRS, g % 2
                wait(dve, exp_done[1], g - 1, turn, LOOP)
                if n == 0:
                    wait(dve, row_scaled, 2 * b + 2, turn, 4)

                def mask_rows(h, t):
                    lo, hi = ((0, P), (P, BLOCKS))[t]
                    return V.tensor_tensor_reduce(ps_s[h][:, lo:hi], ps_s[h][:, lo:hi], mask[:, lo:hi],
                                                  1.0, MASKED, ALU.add, ALU.max, top[i][:, h, t:t + 1])

                def take_shift(h):
                    dve.wait_ge(top_made, count(2 * g + h + 1, turn, 2 * LOOP))
                    V.scalar_tensor_tensor(shift[i][:, h, :], top[i][:, h, :], -SCALE,
                                           row_d[b % 2][:, :, 2 * n + h], ALU.mult, ALU.add)\
                        .then_inc(shift_made, 1)

                wait(dve, s_done[0], g + 1, turn, LOOP)
                dve.sem_inc(waits_over, 1)
                mask_rows(0, 0)
                mask_rows(0, 1).then_inc(top_made, 1)
                wait(dve, s_done[1], g + 1, turn, LOOP)
                dve.sem_inc(waits_over, 1)
                mask_rows(1, 0)
                take_shift(0)
                mask_rows(1, 1).then_inc(top_made, 1)
                if is_pair(g + 1):
                    split_projected(g + 1, turn)
                take_shift(1)

            def round_projected(g, turn):
                i = g % 2
                wait(dve, t_kept, g + 1, turn, LOOP)
                wait(dve, s_done[1], g - 1, turn, LOOP)
                V.tensor_copy(t_hi[i][:], t_sb[i][:, :, P:SEQ]).then_inc(t_rounded, 1)

            def split_projected(g, turn):
                i = g % 2
                wait(dve, t_rounded, g + 1, turn, LOOP)
                V.tensor_tensor(t_lo[i][:], t_sb[i][:, :, P:SEQ], t_hi[i][:].bitcast(f32), ALU.subtract)\
                    .then_inc(t_split, 1)

            def row_stats(b, turn):
                wait(dve, x_in[b % 2], 16 * (b // 2 + 1), turn, 16)
                wait(dve, xn_made, b, turn, 2)
                for t in range(QT):
                    last = V.bn_stats(stats[:, t, :], xin[b % 2][:, t, :])
                last.then_inc(bn_stats_made, 1)
                wait(dve, bn_stats_made, b + 1, turn, 2)
                dve.sem_inc(waits_over, 1)
                for t in range(QT):
                    last = V.bn_aggr(mv[:, t, :], stats[:, t, :])
                last.then_inc(stats_made, 1)

            def normalize(b, turn):
                wait(dve, rstd_made, b + 1, turn, 2)
                wait(dve, stats_made, b + 1, turn, 2)
                wait(dve, xt_done, b, turn, 2)
                for t in range(QT):
                    last = V.tensor_scalar(xn[:, t, :], xin[b % 2][:, t, :], mv[:, t, 0:1], rstd[:, t:t + 1],
                                           ALU.subtract, ALU.mult)
                last.then_inc(xn_made, 1)

            def keep_xt(b, turn):
                i = b % 2
                wait(dve, xt_done, b + 1, turn, 2)
                wait(dve, s_done[1], PAIRS * (b - 1), turn, LOOP)
                V.tensor_copy(xt_f[i][:], ps_x[:, 0:SEQ]).then_inc(xt_kept, 1)
                wait(dve, xt_kept, 2 * b + 1, turn, 4)
                V.tensor_copy(xt_hi[i][:], xt_f[i][:]).then_inc(xt_kept, 1)
                wait(dve, xt_kept, 2 * b + 2, turn, 4)
                V.tensor_tensor(xt_lo[i][:], xt_f[i][:], xt_hi[i][:].bitcast(f32), ALU.subtract)\
                    .then_inc(xt_split, 1)

            def keep_row_bias(b, turn):
                i = b % 2
                wait(dve, row_done, b + 1, turn, 2)
                if b >= 2:
                    wait(dve, shift_made, 2 * PAIRS * (b - 1), turn, 2 * LOOP)
                V.tensor_tensor(row_b[:], ps_x[:, 0:QT * HEADS].rearrange("p (t h) -> p t h", t=QT),
                                bqbk_sum[:], ALU.add).then_inc(row_kept, 1)
                wait(dve, row_kept, b + 1, turn, 2)
                V.tensor_scalar(row_bs[:], row_b[:], SCALE, None, ALU.mult).then_inc(row_scaled, 1)
                wait(dve, row_scaled, 2 * b + 1, turn, 4)
                V.scalar_tensor_tensor(row_d[i][:], row_b[:], -SCALE, row_bs[:], ALU.mult, ALU.add)\
                    .then_inc(row_scaled, 1)

            def keep_values(b, j, turn):
                t, c = j // (E // VH), j % (E // VH)
                wait(dve, v_done, VQ * b + j + 1, turn, 2 * VQ)
                wait(dve, pv_done, TWOS * (b - 1), turn, 2 * TWOS)
                V.tensor_tensor(v_sb[b % 2][:, t, c * VH:(c + 1) * VH], v_bank(b)[:], bv_b[:, c * VH:(c + 1) * VH],
                                ALU.add).then_inc(v_kept, 1)

            def split_attended(g, turn):
                i = g // 2 % 2
                wait(dve, at_rounded, g // 2 + 1, turn, LOOP // 2)
                wait(dve, wo_done, g // 2 - 1, turn, LOOP // 2)
                V.tensor_tensor(at_lo[i][:].rearrange("p j q -> p (j q)"), ps_o[:],
                                at_hi[i][:].bitcast(f32).rearrange("p j q -> p (j q)"), ALU.subtract)\
                    .then_inc(at_split, 1)

            def round_leaves(b, turn):
                wait(dve, leaft_kept, b + 1, turn, 2)
                wait(dve, leaves_done, b, turn, 2)
                V.tensor_copy(leaf_hi[:], leaf_t[:]).then_inc(leaft_rounded, 1)

            def split_leaves(b, turn):
                wait(dve, leaft_rounded, b + 1, turn, 2)
                V.tensor_tensor(leaf_lo[:], leaf_t[:], leaf_hi[:].bitcast(f32), ALU.subtract)\
                    .then_inc(leaft_split, 1)

            def finish(b, turn):
                wait(dve, out_done, b + 1, turn, 2)
                wait(dve, res_made, b + 1, turn, 2)
                r = res[b % 2][:].rearrange("p t m -> p (t m)")
                V.tensor_tensor(r, ps_w[:, 0:QT * DM], r, ALU.add).then_inc(out_made, 1)

            def slot(g, turn):
                b, n = g // PAIRS, g % PAIRS
                if is_pair(g - 1):
                    invert_totals(g - 1, turn)
                if is_pair(g + 1):
                    round_projected(g + 1, turn)
                if n == SUM_SLOT + 1 and is_row(b - 1):
                    finish(b - 1, turn)
                if is_pair(g):
                    mask_and_shift(g, turn)
                elif is_pair(g + 1):
                    split_projected(g + 1, turn)
                if (g - O_LAG) % 2 == 0 and is_pair(g - O_LAG):
                    split_attended(g - O_LAG, turn)
                if is_pair(g - T_LAG):
                    keep_transposed(g - T_LAG, turn)
                if n == 0 and is_row(b + 1):
                    row_stats(b + 1, turn)
                if n == 1 and is_row(b + 1):
                    normalize(b + 1, turn)
                if n == 2 and is_row(b - 1):
                    round_leaves(b - 1, turn)
                if n == 2 and is_row(b + 1):
                    keep_xt(b + 1, turn)
                if n == 2 and is_row(b - 1):
                    split_leaves(b - 1, turn)
                if n == 3 and is_row(b + 1):
                    keep_row_bias(b + 1, turn)
                if n >= VQ and 0 < b + 1 < BATCH:
                    keep_values(b + 1, n - VQ, turn)
                if g == 1:
                    split_a(2)
                    split_a(3)
                if g == 2:
                    dve.wait_ge(lw_kept, 1)
                    V.tensor_copy(lw_hi[:], lw[:]).then_inc(lw_rounded, 1)
                    split_weights(lw_hi[:], lw_lo[:], lw[:], lw_rounded, lw_split)
                if g == 3:
                    split_out_weights()
                if 0 <= g < VQ:
                    keep_values(0, g, None)

            V.memset(rt[:, NODES:LEAVES], 0.0)
            V.memset(ones[:], 1.0).then_inc(const_set, 1)
            row_stats(0, None)
            lay_biases_by_head()
            normalize(0, None)
            keep_xt(0, None)
            split_a(0)
            split_a(1)
            keep_query_bias()
            split_weights(wv_hi[:], wv_lo[:], wv_f[:], wv_rounded, wv_split)
            keep_key_bias()
            keep_row_bias(0, None)
            split_weights(rw_hi[:], rw_lo[:], ps_w[:, 0:LEAVES], rw_rounded, rw_split)
            dve.wait_ge(mask_made, 1)
            run(dve, slot)

        @block.scalar
        def _(act):
            A = nc.scalar

            def round_a(n):
                h = a_heads(n)
                act.wait_ge(a_made, n + 1)
                A.activation(a_hi[:, h, :], a_banks[n][:].rearrange("p (h m) -> p h m", m=DM), ACT.Copy)\
                    .then_inc(a_rounded, 1)

            def round_rw():
                act.wait_ge(rw_made, 1)
                A.activation(rw_hi[:], ps_w[:, 0:LEAVES], ACT.Copy).then_inc(rw_rounded, 1)

            def keep_lw():
                act.wait_ge(lw_made, 1)
                A.activation(lw[:].rearrange("p c m -> p (c m)"), ps_x[:, 0:LC * DM], ACT.Copy,
                             scale=float(0.5 ** DEPTH)).then_inc(lw_kept, 1)

            def round_out_weights():
                act.wait_ge(loaded_out, 3 * 16)
                A.activation(wo_hi[:], wo_f[:], ACT.Copy).then_inc(wo_rounded, 1)

            def keep_transposed(g, h, turn):
                wait(act, pt_done[h], g + 1, turn, LOOP)
                wait(act, pv_done, g // 2 - 1, turn, LOOP // 2)
                A.activation(pt_sb[g % PBUF][:, h, :], ps_p[h][:, 0:BLOCKS], ACT.Copy).then_inc(pt_kept[h], 1)

            def exponentials(g, turn):
                i = g % 2
                wait(act, pt_done[1], g - PBUF + 1, turn, LOOP)
                wait(act, inv_made, g - 1, turn, LOOP)
                for h in range(2):
                    act.wait_ge(shift_made, count(2 * g + h + 1, turn, 2 * LOOP))
                    for t, (lo, hi) in enumerate(((0, P), (P, BLOCKS))):
                        last = A.activation(p_sb[g % PBUF][:, h, lo:hi], ps_s[h][:, lo:hi], ACT.Exp,
                                            bias=shift[i][:, h, t:t + 1], scale=SCALE,
                                            accum_out=total[i][:, h, t:t + 1])
                    last.then_inc(exp_done[h], 1)

            def keep_projected(g, turn):
                n = g % PAIRS
                wait(act, t_done, g + 1, turn, LOOP)
                wait(act, s_done[1], g - 1, turn, LOOP)
                for h in range(2):
                    last = A.activation(t_sb[g % 2][:, h, :], ps_t[:, h * SEQ:(h + 1) * SEQ], ACT.Identity,
                                        bias=query_bias[:, 2 * n + h:2 * n + h + 1])
                last.then_inc(t_kept, 1)

            def round_attended(g, turn):
                wait(act, pv_done, g // 2 + 1, turn, LOOP // 2)
                wait(act, wo_done, g // 2 - 1, turn, LOOP // 2)
                A.activation(at_hi[g // 2 % 2][:].rearrange("p j q -> p (j q)"), ps_o[:], ACT.Copy)\
                    .then_inc(at_rounded, 1)

            def keep_sum(b, turn):
                wait(act, wo_done, TWOS * (b + 1), turn, 2 * TWOS)
                wait(act, out_done, b, turn, 2)
                A.activation(sum_t[:], ps_w[:, 0:SEQ], ACT.Copy).then_inc(sum_kept, 1)

            def gates(b, turn):
                wait(act, logits_done, b + 1, turn, 2)
                wait(act, branch_made, b, turn, 2)
                A.activation(th[:].rearrange("p t n -> p (t n)"), ps_x[:], ACT.Tanh, scale=0.5)\
                    .then_inc(tanh_made, 1)

            def keep_leaves(b, turn):
                wait(act, leaft_done, b + 1, turn, 2)
                wait(act, leaft_split, b, turn, 2)
                A.activation(leaf_t[:].rearrange("p c q -> p (c q)"), ps_x[:], ACT.Copy).then_inc(leaft_kept, 1)

            def slot(g, turn):
                b, n = g // PAIRS, g % PAIRS
                if n == SUM_SLOT and is_row(b - 1):
                    keep_sum(b - 1, turn)
                if is_pair(g):
                    exponentials(g, turn)
                if g == FIRST + 1:
                    round_rw()
                if is_pair(g + 2):
                    keep_projected(g + 2, turn)
                if is_pair(g - T_LAG):
                    keep_transposed(g - T_LAG, 1, turn)
                if (g - V_LAG) % 2 == 0 and is_pair(g - V_LAG):
                    round_attended(g - V_LAG, turn)
                if n == 0 and is_row(b):
                    gates(b, turn)
                if n == 1 and is_row(b - 1):
                    keep_leaves(b - 1, turn)
                if g == 0:
                    round_a(2)
                    round_a(3)
                if g == 2:
                    round_out_weights()
                if g == 1:
                    keep_lw()

            round_a(0)
            round_a(1)
            act.wait_ge(loaded_v, 2 * 16)
            A.activation(wv_hi[:], wv_f[:], ACT.Copy).then_inc(wv_rounded, 1)
            act.wait_ge(biases_kept, 1)
            run(act, slot)

        @block.gpsimd
        def _(pool):
            G = nc.gpsimd

            G.memset(ident[:], 0.0)
            G.memset(minus_half[:], -0.5)
            G.memset(eps[:], EPS).then_inc(const_set, 1)
            G.memset(by_head[:], 0.0).then_inc(zeros_set, 1)
            pool.wait_ge(const_set, 2)
            G.affine_select(out=ident[:], in_=ident[:], compare_op=ALU.not_equal, fill=1.0, base=0,
                            pattern=[[-1, P]], channel_multiplier=1).then_inc(ident_made, 1)

            def make_mask():
                G.memset(mask[:], 0.0).then_inc(zeros_set, 1)
                pool.wait_ge(zeros_set, 2)
                G.affine_select(out=mask[:, 0:P], in_=mask[:, 0:P], compare_op=ALU.is_ge, fill=MASKED, base=0,
                                pattern=[[-1, P]], channel_multiplier=1)
                G.affine_select(out=mask[:, 2 * P:3 * P], in_=mask[:, 2 * P:3 * P], compare_op=ALU.is_ge,
                                fill=MASKED, base=0, pattern=[[-1, P]], channel_multiplier=1)\
                    .then_inc(mask_made, 1)

            def scale_probabilities(g, turn):
                wait(pool, inv_made, g + 1, turn, LOOP)
                p, r = p_sb[g % PBUF], inv[g % 2]
                for t, (lo, hi) in enumerate(((0, P), (P, BLOCKS))):
                    last = G.tensor_tensor(p[:, :, lo:hi], p[:, :, lo:hi],
                                           r[:, :, t:t + 1].to_broadcast([P, 2, hi - lo]), ALU.mult)
                last.then_inc(p_scaled, 1)

            def reciprocal_deviation(b, turn):
                wait(pool, stats_made, b + 1, turn, 2)
                wait(pool, xn_made, b, turn, 2)
                G.tensor_tensor(var_eps[:], mv[:, :, 1], eps[:], ALU.add).then_inc(var_made, 1)
                wait(pool, var_made, b + 1, turn, 2)
                G.tensor_tensor(rstd[:], var_eps[:], minus_half[:], ALU.pow).then_inc(rstd_made, 1)

            def branches(b, turn):
                wait(pool, tanh_made, b + 1, turn, 2)
                one = ones[:, 0:1, None].to_broadcast([P, QT, LEAVES])
                G.tensor_tensor(branch[:, :, :, 0], one, th[:], ALU.subtract)
                G.tensor_tensor(branch[:, :, :, 1], one, th[:], ALU.add).then_inc(branch_made, 1)

            def tree_levels(b, levels, turn):
                for level in levels:
                    n = 2 ** level
                    if level == 1:
                        wait(pool, branch_made, b + 1, turn, 2)
                        parent = branch[:, :, 0, :]
                        wait(pool, leaft_done, b, turn, 2)
                    else:
                        parent = prob[level % 2][:, :, 0:n]
                        pool.wait_ge(level_made, count((DEPTH - 2) * b + level - 1, turn, 2 * (DEPTH - 2)))
                    last = G.tensor_tensor(
                        prob[(level + 1) % 2][:, :, 0:2 * n].rearrange("p t (n c) -> p t n c", c=2),
                        parent[:, :, :, None].to_broadcast([P, QT, n, 2]),
                        branch[:, :, n - 1:2 * n - 1, :], ALU.mult)
                    if level < DEPTH - 1:
                        last.then_inc(level_made, 1)
                    else:
                        last.then_inc(leaf_made, 1)

            def residual(b, turn):
                wait(pool, x_in[b % 2], 16 * (b // 2 + 1), turn, 16)
                wait(pool, xn_made, b + 1, turn, 2)
                if b == 0:
                    pool.wait_ge(out_bias_made, 1)
                wait(pool, stored[b % 2], 16 * (b // 2), turn, 16)
                G.tensor_tensor(res[b % 2][:], xin[b % 2][:],
                                out_bias[:, None, :].to_broadcast([P, QT, DM]), ALU.add).then_inc(res_made, 1)

            def slot(g, turn):
                b, n = g // PAIRS, g % PAIRS
                if is_pair(g - 1):
                    scale_probabilities(g - 1, turn)
                if n == 0 and is_row(b + 1):
                    reciprocal_deviation(b + 1, turn)
                if n == 1 and is_row(b):
                    branches(b, turn)
                if n == 2 and is_row(b):
                    tree_levels(b, range(1, 5), turn)
                if n == 3 and is_row(b):
                    tree_levels(b, range(5, DEPTH), turn)
                if g == 4:
                    residual(0, None)
                if n == 7 and 0 < b + 1 < BATCH:
                    residual(b + 1, turn)

            reciprocal_deviation(0, None)
            make_mask()
            run(pool, slot)


def kernel(**inputs):
    import numpy as np
    import concourse.bacc as bacc
    from concourse.bass_utils import run_bass_kernel_spmd

    def given(name):
        return np.asarray(inputs[name])

    def by_pairs(w):
        heads, model, dims = w.shape
        return w.transpose(0, 2, 1).reshape(heads // 2, 2 * dims, model).transpose(1, 0, 2)

    def bias_by_pairs(b):
        heads, dims = b.shape
        return b.reshape(heads // 2, 2 * dims).T

    laid_out = {
        "x": given("L0_attn_residual"),
        "wq_t": by_pairs(given("L0_attn_W_Q")),
        "wk_t": by_pairs(given("L0_attn_W_K")),
        "wv": given("L0_attn_W_V"),
        "wo": given("L0_attn_W_O"),
        "bq_t": bias_by_pairs(given("L0_attn_b_Q")),
        "bk_t": bias_by_pairs(given("L0_attn_b_K")),
        "bv": given("L0_attn_b_V"),
        "bo": given("L0_attn_b_O"),
        "ffn_wq": given("L0_ffn_Wq"),
        "routers_t": given("L0_ffn_routers").T,
        "leaf_values_t": given("L0_ffn_leaf_values").T,
        "wout_t": given("L0_ffn_Wout_w").T,
        "wout_b": given("L0_ffn_Wout_b"),
    }
    nc = bacc.Bacc("TRN2", target_bir_lowering=False, num_devices=1)
    arrays, args = {}, []
    for name, a in laid_out.items():
        a = np.ascontiguousarray(a)
        arrays[f"in_{name}"] = a
        args.append(nc.dram_tensor(f"in_{name}", a.shape, mybir.dt.from_np(a.dtype), kind="ExternalInput").ap())
    out = nc.dram_tensor("out", laid_out["x"].shape, mybir.dt.float32, kind="ExternalOutput").ap()
    attention_and_tree_ffn(nc, *args, out)
    result = run_bass_kernel_spmd(nc, [arrays], core_ids=[0])
    return result.results[0]["out"]
```
